# Optimizing a Trainium2 kernel written in Bass

```python
import numpy as np
import jax
import jax.numpy as jnp

def _softmax(x, axis=-1):
    return jax.nn.softmax(x, axis=axis)

def _gelu(x):
    return jax.nn.gelu(x, approximate=True)

def _silu(x):
    return jax.nn.silu(x)

def _sigmoid(x):
    return jax.nn.sigmoid(x)

def _layernorm(x, axis=-1, eps=1e-05):
    m = jnp.mean(x, axis=axis, keepdims=True)
    v = jnp.var(x, axis=axis, keepdims=True)
    return (x - m) / jnp.sqrt(v + eps)

def _scatter_add(tgt, idx, src, axis=0):
    return tgt.at[idx].add(src)

def _segment_sum(src, seg, n):
    return jax.ops.segment_sum(src, seg, n)
kernel_name = 'mk_vit_tower_d1_tok_img256_r4_895a62'

def setup_inputs(seed: int=0):
    np.random.seed(seed)
    _w = jnp.asarray

    def _rec_inputs():
        import jax
        import jax.numpy as jnp
        _rk = jax.random.key(seed)
        x = -0.000125008 + 0.999885 * jax.random.normal(jax.random.fold_in(_rk, 1), (32, 64, 64, 64), jnp.float32)
        return x
    x = _rec_inputs()

    def _L0_tok_setup():
        import jax, jax.numpy as jnp
        import numpy as np
        B, D, H, W = (32, 64, 64, 64)
        KEEP_RATIO = 0.5
        LN_EPS = 1e-05
        key = jax.random.key(seed)
        k1, k2 = jax.random.split(key)
        return {'tokens': jax.random.normal(k1, (B, D, H, W), dtype=jnp.float32), 'norm_w': jnp.ones((D,), dtype=jnp.float32), 'norm_b': jnp.zeros((D,), dtype=jnp.float32), 'fc_w': jax.random.normal(k2, (1, D), dtype=jnp.float32) * (1.0 / np.sqrt(D)), 'fc_b': jnp.zeros((1,), dtype=jnp.float32)}
    _L0_tok_all = _L0_tok_setup()
    _L0_tok_in = {k: v for k, v in _L0_tok_all.items() if k in ('norm_w', 'norm_b', 'fc_w', 'fc_b')}
    del _L0_tok_all

    def _L0_attn_setup():
        import jax, jax.numpy as jnp
        import numpy as np
        MEMORY_SIZE = 40
        INPUT_SIZE = 64
        OUTPUT_SIZE = 64
        BATCH = 16
        SEQ = 1024
        key = jax.random.key(seed)
        k1, k2, k3, k4 = jax.random.split(key, 4)
        x = jax.random.normal(k1, (BATCH, SEQ, INPUT_SIZE), dtype=jnp.float32)
        lim_w = float(np.sqrt(6.0 / (INPUT_SIZE + OUTPUT_SIZE)))
        W1 = jax.random.uniform(k2, (INPUT_SIZE, OUTPUT_SIZE), minval=-lim_w, maxval=lim_w, dtype=jnp.float32)
        W2 = jax.random.uniform(k3, (INPUT_SIZE, OUTPUT_SIZE), minval=-lim_w, maxval=lim_w, dtype=jnp.float32)
        bias = jnp.ones((OUTPUT_SIZE,), dtype=jnp.float32)
        lim_m = float(np.sqrt(6.0 / (MEMORY_SIZE + 1 + INPUT_SIZE)))
        mw = jax.random.uniform(k4, (MEMORY_SIZE + 1, INPUT_SIZE), minval=-lim_m, maxval=lim_m, dtype=jnp.float32)
        mw = mw.at[0].set(0.0)
        return {'input_data': x, 'W1': W1, 'W2': W2, 'bias': bias, 'memory_weights': mw}
    _L0_attn_all = _L0_attn_setup()
    _L0_attn_in = {k: v for k, v in _L0_attn_all.items() if k in ('W1', 'W2', 'bias', 'memory_weights')}
    del _L0_attn_all

    def _L0_ffn_setup():
        import jax, jax.numpy as jnp
        import numpy as np
        B, N, D = (16, 1024, 64)
        NUM_EXPERTS, TOP_K, HEADS = (4, 2, 4)
        N_EDGES = 262144
        LN_EPS = 1e-05

        def _layernorm(x, g, b):
            mu = x.mean(-1, keepdims=True)
            var = ((x - mu) ** 2).mean(-1, keepdims=True)
            return (x - mu) * jax.lax.rsqrt(var + LN_EPS) * g + b

        def _forward(x, edge_index, W_gat, att_src, att_dst, b_gat, ln_gamma, ln_beta, W1, b1, W2, b2):
            Bc, Nc, Dc = x.shape
            M = Bc * Nc
            x_flat = x.reshape(M, Dc)
            h = (x_flat @ W_gat).reshape(M, HEADS, NUM_EXPERTS)
            loops = jnp.arange(M, dtype=edge_index.dtype)
            src = jnp.concatenate([edge_index[0], loops])
            dst = jnp.concatenate([edge_index[1], loops])
            a_src = (h * att_src).sum(-1)
            a_dst = (h * att_dst).sum(-1)
            e = jax.nn.leaky_relu(a_src[src] + a_dst[dst], negative_slope=0.2)
            e_max = jax.ops.segment_max(e, dst, num_segments=M)
            ee = jnp.exp(e - e_max[dst])
            denom = jax.ops.segment_sum(ee, dst, num_segments=M)
            alpha = ee / (denom[dst] + 1e-16)
            msg = h[src] * alpha[:, :, None]
            agg = jax.ops.segment_sum(msg, dst, num_segments=M).reshape(M, HEADS * NUM_EXPERTS) + b_gat
            scores = _layernorm(agg, ln_gamma, ln_beta).reshape(M, HEADS, NUM_EXPERTS).mean(1)
            scores = scores.reshape(Bc, Nc, NUM_EXPERTS)
            topk_s, topk_i = jax.lax.top_k(scores, TOP_K)
            w = jax.nn.softmax(topk_s, axis=-1)
            out = jnp.zeros_like(x)
            for ei in range(NUM_EXPERTS):
                g = jnp.where(topk_i == ei, w, 0.0).sum(-1)
                hh = jax.nn.gelu(x @ W1[ei] + b1[ei], approximate=False)
                out = out + g[..., None] * (hh @ W2[ei] + b2[ei])
            return out
        key = jax.random.key(seed)
        ks = jax.random.split(key, 8)
        s = 0.05
        return {'x': jax.random.normal(ks[0], (B, N, D), jnp.float32), 'W_gat': jax.random.normal(ks[1], (D, HEADS * NUM_EXPERTS), jnp.float32) * s, 'att_src': jax.random.normal(ks[2], (HEADS, NUM_EXPERTS), jnp.float32) * s, 'att_dst': jax.random.normal(ks[3], (HEADS, NUM_EXPERTS), jnp.float32) * s, 'b_gat': jnp.zeros((HEADS * NUM_EXPERTS,), jnp.float32), 'ln_gamma': jnp.ones((HEADS * NUM_EXPERTS,), jnp.float32), 'ln_beta': jnp.zeros((HEADS * NUM_EXPERTS,), jnp.float32), 'W1': jax.random.normal(ks[4], (NUM_EXPERTS, D, 2 * D), jnp.float32) * s, 'b1': jnp.zeros((NUM_EXPERTS, 2 * D), jnp.float32), 'W2': jax.random.normal(ks[5], (NUM_EXPERTS, 2 * D, D), jnp.float32) * s, 'b2': jnp.zeros((NUM_EXPERTS, D), jnp.float32), 'edge_index': jax.random.randint(ks[6], (2, N_EDGES), 0, B * N, jnp.int32)}
    _L0_ffn_all = _L0_ffn_setup()
    _L0_ffn_in = {k: v for k, v in _L0_ffn_all.items() if k in ('W_gat', 'att_src', 'att_dst', 'b_gat', 'ln_gamma', 'ln_beta', 'W1', 'b1', 'W2', 'b2', 'edge_index')}
    del _L0_ffn_all
    return {'x': x, 'L0_tok_norm_w': _L0_tok_in['norm_w'], 'L0_tok_norm_b': _L0_tok_in['norm_b'], 'L0_tok_fc_w': _L0_tok_in['fc_w'], 'L0_tok_fc_b': _L0_tok_in['fc_b'], 'L0_attn_W1': _L0_attn_in['W1'], 'L0_attn_W2': _L0_attn_in['W2'], 'L0_attn_bias': _L0_attn_in['bias'], 'L0_attn_memory_weights': _L0_attn_in['memory_weights'], 'L0_ffn_W_gat': _L0_ffn_in['W_gat'], 'L0_ffn_att_src': _L0_ffn_in['att_src'], 'L0_ffn_att_dst': _L0_ffn_in['att_dst'], 'L0_ffn_b_gat': _L0_ffn_in['b_gat'], 'L0_ffn_ln_gamma': _L0_ffn_in['ln_gamma'], 'L0_ffn_ln_beta': _L0_ffn_in['ln_beta'], 'L0_ffn_W1': _L0_ffn_in['W1'], 'L0_ffn_b1': _L0_ffn_in['b1'], 'L0_ffn_W2': _L0_ffn_in['W2'], 'L0_ffn_b2': _L0_ffn_in['b2'], 'L0_ffn_edge_index': _L0_ffn_in['edge_index']}

def reference(x, L0_tok_norm_w, L0_tok_norm_b, L0_tok_fc_w, L0_tok_fc_b, L0_attn_W1, L0_attn_W2, L0_attn_bias, L0_attn_memory_weights, L0_ffn_W_gat, L0_ffn_att_src, L0_ffn_att_dst, L0_ffn_b_gat, L0_ffn_ln_gamma, L0_ffn_ln_beta, L0_ffn_W1, L0_ffn_b1, L0_ffn_W2, L0_ffn_b2, L0_ffn_edge_index):
    import jax
    import jax.numpy as jnp

    def _L0_tok_ref(tokens, norm_w, norm_b, fc_w, fc_b):
        import jax, jax.numpy as jnp
        import numpy as np
        B, D, H, W = (32, 64, 64, 64)
        KEEP_RATIO = 0.5
        LN_EPS = 1e-05
        b, d, h, w = tokens.shape
        n = h * w
        num_keep = int(n * KEEP_RATIO)
        t = tokens.transpose(0, 2, 3, 1).reshape(b, n, d)
        mu = jnp.mean(t, axis=-1, keepdims=True)
        var = jnp.mean(jnp.square(t - mu), axis=-1, keepdims=True)
        ln = (t - mu) * jax.lax.rsqrt(var + LN_EPS) * norm_w + norm_b
        scores = jnp.einsum('bnd,d->bn', ln, fc_w[0]) + fc_b[0]
        scores = jax.nn.softmax(scores, axis=-1)
        _, idx = jax.lax.top_k(scores, num_keep)
        idx = jnp.sort(idx, axis=-1)
        selected = jnp.take_along_axis(t, idx[:, :, None], axis=1)
        return selected

    def _L0_attn_ref(input_data, W1, W2, bias, memory_weights):
        import jax, jax.numpy as jnp
        import numpy as np
        MEMORY_SIZE = 40
        INPUT_SIZE = 64
        OUTPUT_SIZE = 64
        BATCH = 16
        SEQ = 1024
        m = memory_weights.shape[0] - 1
        B, T, D = input_data.shape
        total = jnp.sum(input_data, axis=1, keepdims=True)
        h_hatt = jnp.zeros_like(input_data)
        win = jnp.zeros_like(input_data)
        for l in range(1, m + 1):
            shifted = jnp.pad(input_data[:, :T - l], ((0, 0), (l, 0), (0, 0)))
            h_hatt = h_hatt + memory_weights[l] * shifted
            win = win + shifted
        h_hatt = h_hatt + memory_weights[0] * (total - win)
        return input_data @ W1 + h_hatt @ W2 + bias

    def _L0_ffn_ref(x, W_gat, att_src, att_dst, b_gat, ln_gamma, ln_beta, W1, b1, W2, b2, edge_index):
        import jax, jax.numpy as jnp
        import numpy as np
        B, N, D = (16, 1024, 64)
        NUM_EXPERTS, TOP_K, HEADS = (4, 2, 4)
        N_EDGES = 262144
        LN_EPS = 1e-05

        def _layernorm(x, g, b):
            mu = x.mean(-1, keepdims=True)
            var = ((x - mu) ** 2).mean(-1, keepdims=True)
            return (x - mu) * jax.lax.rsqrt(var + LN_EPS) * g + b

        def _forward(x, edge_index, W_gat, att_src, att_dst, b_gat, ln_gamma, ln_beta, W1, b1, W2, b2):
            Bc, Nc, Dc = x.shape
            M = Bc * Nc
            x_flat = x.reshape(M, Dc)
            h = (x_flat @ W_gat).reshape(M, HEADS, NUM_EXPERTS)
            loops = jnp.arange(M, dtype=edge_index.dtype)
            src = jnp.concatenate([edge_index[0], loops])
            dst = jnp.concatenate([edge_index[1], loops])
            a_src = (h * att_src).sum(-1)
            a_dst = (h * att_dst).sum(-1)
            e = jax.nn.leaky_relu(a_src[src] + a_dst[dst], negative_slope=0.2)
            e_max = jax.ops.segment_max(e, dst, num_segments=M)
            ee = jnp.exp(e - e_max[dst])
            denom = jax.ops.segment_sum(ee, dst, num_segments=M)
            alpha = ee / (denom[dst] + 1e-16)
            msg = h[src] * alpha[:, :, None]
            agg = jax.ops.segment_sum(msg, dst, num_segments=M).reshape(M, HEADS * NUM_EXPERTS) + b_gat
            scores = _layernorm(agg, ln_gamma, ln_beta).reshape(M, HEADS, NUM_EXPERTS).mean(1)
            scores = scores.reshape(Bc, Nc, NUM_EXPERTS)
            topk_s, topk_i = jax.lax.top_k(scores, TOP_K)
            w = jax.nn.softmax(topk_s, axis=-1)
            out = jnp.zeros_like(x)
            for ei in range(NUM_EXPERTS):
                g = jnp.where(topk_i == ei, w, 0.0).sum(-1)
                hh = jax.nn.gelu(x @ W1[ei] + b1[ei], approximate=False)
                out = out + g[..., None] * (hh @ W2[ei] + b2[ei])
            return out
        return _forward(x, edge_index, W_gat, att_src, att_dst, b_gat, ln_gamma, ln_beta, W1, b1, W2, b2)
    h = _L0_tok_ref(x, L0_tok_norm_w, L0_tok_norm_b, L0_tok_fc_w, L0_tok_fc_b)
    h = h + _L0_attn_ref(_layernorm(h, axis=-1), L0_attn_W1, L0_attn_W2, L0_attn_bias, L0_attn_memory_weights)
    h = h + _L0_ffn_ref(_layernorm(h, axis=-1), L0_ffn_W_gat, L0_ffn_att_src, L0_ffn_att_dst, L0_ffn_b_gat, L0_ffn_ln_gamma, L0_ffn_ln_beta, L0_ffn_W1, L0_ffn_b1, L0_ffn_W2, L0_ffn_b2, L0_ffn_edge_index)
    return h

_drawn_inputs = setup_inputs


def setup_inputs(seed=0):
    import zlib

    import numpy as np

    out = dict(_drawn_inputs(seed))
    spreads = {'L0_tok_norm_w': (1.0, 0.2),
     'L0_tok_norm_b': (0.0, 0.1),
     'L0_attn_bias': (1.0, 0.2),
     'L0_ffn_b_gat': (0.0, 0.33),
     'L0_ffn_ln_gamma': (1.0, 0.6),
     'L0_ffn_ln_beta': (0.0, 0.633),
     'L0_ffn_b1': (0.0, 0.722),
     'L0_ffn_b2': (0.0, 0.1)}
    factors = {'L0_ffn_att_src': 44.021, 'L0_ffn_att_dst': 64.0}
    for name, (base, spread) in spreads.items():
        noise = np.random.default_rng([zlib.crc32(name.encode()), seed]).standard_normal(out[name].shape)
        drawn = base * np.exp(spread * noise) if base else spread * noise
        out[name] = jnp.asarray(drawn.astype(out[name].dtype))
    for name, factor in factors.items():
        out[name] = (out[name] * factor).astype(out[name].dtype)
    return out
```

```python
import numpy as np
import concourse.bass as bass
from concourse import mybir
from contextlib import ExitStack

F32 = mybir.dt.float32
I32 = mybir.dt.int32
ALU = mybir.AluOpType
ACT = mybir.ActivationFunctionType
AX = mybir.AxisListType.X
U16 = mybir.dt.uint16
BF16 = mybir.dt.bfloat16
LAG_W = 256
M_NODES, N_EDGES = 65536, 262144
COLS = N_EDGES // 128
NODE_TILES = M_NODES // 128
SKIP = 1 << 20
LOW = -1e30


class Chain:

    def __init__(self, eng, sem):
        self.eng, self.sem, self.base, self.n = eng, sem, 0, 0

    def done(self, ins, apart=None):
        ins.then_inc(self.sem, 1)
        self.n += 1
        self.eng.wait_ge(self.sem, self.base + self.n)
        if apart is not None:
            self.eng.sem_inc(apart, 1)

    def start(self, base):
        self.base, self.n = base, 0


def bc(ap, dim, count):
    return ap.unsqueeze(dim).to_broadcast([*ap.shape[:dim], count, *ap.shape[dim:]])


def make_constants(nc, t, dram):
    with ExitStack() as ctx:
        sem = lambda n: ctx.enter_context(nc.semaphore(n))
        sb = lambda n, s, d=F32: ctx.enter_context(nc.sbuf_tensor(n, s, d))
        ps = ctx.enter_context(nc.psum_tensor("prep_psum", [128, 512], F32))
        small_in, built, mean_ready, used, dve = (sem(n) for n in
            ("small_in", "built", "mean_ready", "centred", "prep_dve"))
        rows_out = sem("rows_out")
        raw = sb("raw", [128, 8])
        cols = sb("cols", [128, 4])
        mem_t = sb("mem_t", [64, 41])
        rows = sb("rows", [64, LAG_W])
        wg = sb("wg", [64, 16])
        att = sb("att", [64, 2, 16])
        prod = sb("prod", [64, 2, 16])
        block = ctx.enter_context(nc.Block())

        @block.sync
        def _(sp):
            column = lambda v: v.rearrange("(d one) -> d one", one=1)
            for half in range(2):
                h = slice(64 * half, 64 * half + 64)
                sp.dma_start(raw[h, 0:1], column(dram["norm_w"])).then_inc(small_in, 16)
                sp.dma_start(raw[h, 1:2], column(dram["norm_b"])).then_inc(small_in, 16)
                sp.dma_start(raw[h, 2:3], dram["fc_w"].rearrange("one d -> d one"), allow_slow_non_contiguous=True).then_inc(small_in, 16)
            sp.dma_start(raw[:, 3:4], dram["fc_b"].rearrange("(a b) -> a b", a=1).to_broadcast([128, 1])).then_inc(small_in, 16)
            sp.dma_start(mem_t[:, :], dram["mem"].rearrange("l d -> d l"), allow_slow_non_contiguous=True).then_inc(small_in, 16)
            sp.dma_start(wg[:, :], dram["W_gat"]).then_inc(small_in, 16)
            for k, name in enumerate(("att_src", "att_dst")):
                sp.dma_start(att[:, k, :], dram[name].rearrange("h e -> (h e)").rearrange("(a n) -> a n", a=1)
                             .to_broadcast([64, 16])).then_inc(small_in, 16)
            sp.dma_start(t["w12"][0:64, :], dram["A_W1"]).then_inc(small_in, 16)
            sp.dma_start(t["w12"][64:128, :], dram["A_W2"]).then_inc(small_in, 16)
            sp.dma_start(t["bias4"][:, :].rearrange("a (r n) -> a r n", r=4),
                         bc(dram["A_bias"].rearrange("(a n) -> a n", a=1), 1, 4)).then_inc(small_in, 16)
            sp.dma_start(t["m0"][64:128, :], dram["mem"][0, :].rearrange("(d one) -> d one", one=1)).then_inc(small_in, 16)
            sp.wait_ge(dve, 5)
            sp.dma_start(dram["lag_rows"].rearrange("k d x -> d k x"), bc(rows[:, :], 1, 128)).then_inc(rows_out, 16)
            sp.wait_ge(rows_out, 16)

        @block.gpsimd
        def _(pool):
            nc.gpsimd.memset(t["ident"][:, :], 0.0).then_inc(built, 1)
            nc.gpsimd.memset(t["ones"][:, :], 1.0).then_inc(built, 1)
            nc.gpsimd.memset(t["before"][:, :], 1.0).then_inc(built, 1)
            nc.gpsimd.memset(t["halves"][:, :], 0.0).then_inc(built, 1)
            nc.gpsimd.memset(t["stat_w"][:, :], 0.0).then_inc(built, 1)
            pool.wait_ge(built, 5)
            nc.gpsimd.affine_select(out=t["ident"][:, :], in_=t["ident"][:, :], compare_op=ALU.not_equal,
                                    fill=1.0, base=0, pattern=[[-1, 128]], channel_multiplier=1).then_inc(built, 1)
            nc.gpsimd.affine_select(out=t["before"][:, :], in_=t["before"][:, :], compare_op=ALU.is_gt,
                                    fill=0.0, base=0, pattern=[[1, 128]], channel_multiplier=-1).then_inc(built, 1)
            for half in range(2):
                h = slice(64 * half, 64 * half + 64)
                pool.wait_ge(built, 7 + 2 * half)
                nc.gpsimd.memset(t["halves"][h, h], 1.0 / 64).then_inc(built, 1)
                pool.wait_ge(built, 8 + 2 * half)
                nc.gpsimd.memset(t["stat_w"][h, 2 + half:3 + half], 1.0 / 64).then_inc(built, 1)
            pool.wait_ge(built, 11)
            nc.gpsimd.memset(t["reset"][:, :, :], 1.0).then_inc(built, 1)
            pool.wait_ge(built, 12)
            nc.gpsimd.memset(t["reset"][:, :, 0:1], 0.0).then_inc(built, 1)
            nc.gpsimd.iota(t["rowbase"][:, :], pattern=[[2048, 32]], base=0, channel_multiplier=0,
                           allow_small_or_imprecise_dtypes=True).then_inc(built, 1)

        @block.vector
        def _(v):
            ch = Chain(v, dve)
            v.wait_ge(small_in, 16 * 15)
            ch.done(nc.vector.tensor_tensor(cols[:, 0:1], raw[:, 0:1], raw[:, 2:3], ALU.mult))
            ch.done(nc.vector.tensor_tensor(cols[:, 1:2], raw[:, 1:2], raw[:, 2:3], ALU.mult))
            ch.done(nc.vector.memset(rows[:, :], 0.0))
            ch.done(nc.vector.tensor_copy(raw[0:64, 4:5], mem_t[:, 0:1]))
            ch.done(nc.vector.tensor_scalar(rows[:, 128:168], mem_t[:, 1:41], mem_t[:, 0:1], None, ALU.subtract))
            v.wait_ge(mean_ready, 1)
            ch.done(nc.vector.tensor_copy(cols[:, 2:4], ps[:, 0:2]))
            ch.done(nc.vector.tensor_tensor(cols[:, 0:1], cols[:, 0:1], cols[:, 2:3], ALU.subtract))
            ch.done(nc.vector.tensor_tensor(cols[:, 1:2], cols[:, 0:1], cols[:, 0:1], ALU.mult)
                    )
            v.wait_ge(built, 14)
            ch.done(nc.vector.tensor_copy(t["stat_w"][0:64, 0:1], cols[0:64, 0:1]))
            ch.done(nc.vector.tensor_copy(t["stat_w"][64:128, 1:2], cols[64:128, 0:1]))
            ch.done(nc.vector.tensor_scalar(t["bias_s"][:, :], cols[:, 3:4], 64.0, raw[:, 3:4], ALU.mult, ALU.add))
            nc.vector.tensor_copy(cols[:, 2:3], cols[:, 1:2]).then_inc(used, 1)
            v.wait_ge(mean_ready, 2)
            ch.done(nc.vector.tensor_copy(t["bound"][:, :], ps[:, 2:3]))
            ch.done(nc.vector.memset(t["unit"][:, :], 0.0))
            ch.done(nc.vector.memset(t["unit"][:, 0:20].rearrange("p (h v) -> p h v", v=5)[:, :, 0:1], 1.0))
            ch.done(nc.vector.memset(t["w_cat"][:, :], 0.0))
            ch.done(nc.vector.tensor_copy(
                t["w_cat"][:, 0:20].rearrange("d (h v) -> d h v", v=5)[:, :, 1:5],
                wg[:, :].rearrange("d (h v) -> d h v", v=4)))
            ch.done(nc.vector.tensor_tensor(prod[:, :, :], att[:, :, :], bc(wg[:, :], 1, 2), ALU.mult))
            ch.done(nc.vector.tensor_reduce(t["w_cat"][:, 20:28].rearrange("d (k h) -> d k h", k=2),
                                            prod[:, :, :].rearrange("d k (h v) -> d k h v", v=4), AX, ALU.add))

        @block.tensor
        def _(pe):
            pe.wait_ge(built, 14)
            pe.wait_ge(dve, 2)
            nc.tensor.matmul(ps[:, 0:2], t["halves"][:, :], cols[:, 0:2], start=True, stop=True).then_inc(mean_ready, 1)
            pe.wait_ge(used, 1)
            nc.tensor.matmul(ps[:, 2:3], t["halves"][:, :], cols[:, 2:3], start=True, stop=True).then_inc(mean_ready, 1)

        @block.scalar
        def _(act):
            act.wait_ge(dve, 12)
            act.activation(t["bound"][:, :], t["bound"][:, :], ACT.Sqrt, scale=64.0 * 64.0 * 1.01).then_inc(used, 1)
            act.wait_ge(used, 2)


def select_tokens(nc, t, dram):
    x2 = dram["x"].rearrange("(q b) d h w -> q (b d) (h w)", b=2)
    with ExitStack() as ctx:
        sem = lambda n: ctx.enter_context(nc.semaphore(n))
        sb = lambda n, s, d=F32: ctx.enter_context(nc.sbuf_tensor(n, s, d))
        pt = lambda n, s: ctx.enter_context(nc.psum_tensor(n, s, F32))
        ident, ones, before = t["ident"], t["ones"], t["before"]
        xt = [sb(f"image{i}", [128, 4096]) for i in range(2)]
        T = [sb(f"tokens{i}", [128, 8, 32, 64]) for i in range(2)]
        sq = [sb(f"squares{i}", [128, 4, 2, 64]) for i in range(2)]
        idx = [sb(f"place{i}", [128, 256], I32) for i in range(2)]
        big = lambda n: sb(n, [128, 8, 32])
        dot, mu, ss, sc, a1, a2, tie, sel, run = (big(n) for n in
            ("dot", "mu", "ss", "score", "tmp1", "tmp2", "tie", "sel", "run"))
        small = lambda n: sb(n, [128, 8])
        lo, hi, mid, cnt, need, tot = (small(n) for n in ("lo", "hi", "mid", "cnt", "need", "tot"))
        geq = sb("geq", [128, 8], I32)
        lss = sb("lss", [128, 8], I32)
        tp = [pt(f"tp{i}", [128, 4, 2, 64]) for i in range(4)]
        stp = [pt(f"stp{i}", [128, 32, 4]) for i in range(2)]
        cp = pt("cp", [128, 8])
        loaded = [sem("image_in0"), sem("image_in1")]
        image_free, tp_ready, tp_free, st_ready, st_free = (sem(n) for n in
            ("image_free", "tp_ready", "tp_free", "st_ready", "st_free"))
        sq_ready, sq_free, var_ready, std_ready = (sem(n) for n in ("sq_ready", "sq_free", "var_ready", "std_ready"))
        cnt_ready, cnt_out, dve, idx_ready = (sem(n) for n in ("cnt_ready", "cnt_out", "sel_dve", "idx_ready"))
        sent = [sem("kept_out0"), sem("kept_out1")]
        pace, pace_pool = sem("pace"), sem("pace_pool")
        ITER = 32
        PAIRS = 4
        SUMS = ITER + 3
        block = ctx.enter_context(nc.Block())

        def groups(eng):
            with eng.Fori(0, 2) as g2:
                for gb in range(2):
                    yield g2, gb, g2 * 2 + gb

        @block.sync
        def _(sp):
            with sp.Fori(0, 8) as q:
                for qb in range(2):
                    sp.wait_ge(image_free, q * 2 + qb + 1)
                    sp.dma_start(xt[qb][:, :], x2[bass.ds(q * 2 + qb, 1)].rearrange("a p n -> (a p) n")).then_inc(loaded[qb], 16)

        @block.tensor
        def _(pe):
            pe.sem_inc(image_free, 2)
            for g2, gb, g in groups(pe):
                with pe.Fori(0, 2) as q2:
                    for qb in range(2):
                        pair = g * PAIRS + q2 * 2 + qb
                        pe.wait_ge(loaded[qb], (g * 2 + q2 + 1) * 16)
                        xv = xt[qb][:, :].rearrange("p (n c) -> p c n", c=32)
                        for c4 in range(8):
                            pe.wait_ge(tp_free, pair * 8 + c4 + 1)
                            for j in range(4):
                                last = nc.tensor.transpose(tp[c4 % 4][:, j, :, :].rearrange("p b d -> p (b d)"),
                                                           xv[:, c4 * 4 + j, :], ident[:, :])
                            last.then_inc(tp_ready, 1)
                        pe.wait_ge(st_free, pair + 1)
                        for c in range(32):
                            last = nc.tensor.matmul(stp[qb][:, c, :], xv[:, c, :], t["stat_w"][:, :], start=True, stop=True)
                        last.then_inc(st_ready, 1)
                        nc.tensor.matmul(cp[:, 0:1], ones[:, :], ones[:, 0:1], start=True, stop=True).then_inc(image_free, 1)
                with pe.Fori(0, ITER) as i:
                    pe.wait_ge(cnt_ready, g * SUMS + i + 1)
                    nc.tensor.matmul(cp[:, :], ones[:, :], cnt[:, :], start=True, stop=True).then_inc(cnt_out, 1)
                pe.wait_ge(cnt_ready, g * SUMS + ITER + 1)
                nc.tensor.matmul(cp[:, :], ones[:, :], cnt[:, :], start=True, stop=True).then_inc(cnt_out, 1)
                for k in range(2):
                    pe.wait_ge(cnt_ready, g * SUMS + ITER + 2 + k)
                    nc.tensor.matmul(cp[:, :], before[:, :], tot[:, :], start=True, stop=True).then_inc(cnt_out, 1)

        @block.scalar
        def _(act):
            act.sem_inc(tp_free, 4)
            for g2, gb, g in groups(act):
                act.wait_ge(sent[gb], g2 * 4096)
                with act.Fori(0, 2) as q2:
                    for qb in range(2):
                        pair = g * PAIRS + q2 * 2 + qb
                        for c4 in range(8):
                            act.wait_ge(tp_ready, pair * 8 + c4 + 1)
                            act.activation(
                                T[gb][:, bass.ds(q2 * 4 + qb * 2, 2), c4 * 4:c4 * 4 + 4, :].rearrange("p b c d -> p c b d"),
                                tp[c4 % 4][:, :, :, :], ACT.Copy)
                            act.wait_ge(sq_free, pair * 8 + c4 + 1)
                            act.activation(sq[c4 % 2][:, :, :, :], tp[c4 % 4][:, :, :, :], ACT.Square).then_inc(sq_ready, 1)
                            act.wait_ge(sq_ready, pair * 8 + c4 + 1)
                            act.sem_inc(tp_free, 1)
                act.wait_ge(var_ready, g + 1)
                act.activation(a2[:, :, :], a1[:, :, :], ACT.Sqrt).then_inc(std_ready, 1)

        @block.vector
        def _(v):
            v.sem_inc(sq_free, 2)
            v.sem_inc(st_free, 2)
            ch = Chain(v, dve)
            K_ITER, K_REST = 6, 29
            per_group = K_ITER * ITER + K_REST
            for g2, gb, g in groups(v):
                with v.Fori(0, 2) as q2:
                    for qb in range(2):
                        pair = g * PAIRS + q2 * 2 + qb
                        for c4 in range(8):
                            v.wait_ge(sq_ready, pair * 8 + c4 + 1)
                            nc.vector.tensor_reduce(
                                ss[:, bass.ds(q2 * 4 + qb * 2, 2), c4 * 4:c4 * 4 + 4].rearrange("p b c -> p c b"),
                                sq[c4 % 2][:, :, :, :], AX, ALU.add).then_inc(sq_free, 1)
                        v.wait_ge(st_ready, pair + 1)
                        here = bass.ds(q2 * 4 + qb * 2, 2)
                        nc.vector.tensor_copy(dot[:, here, :], stp[qb][:, :, 0:2].rearrange("p c b -> p b c"))
                        nc.vector.tensor_copy(mu[:, here, :], stp[qb][:, :, 2:4].rearrange("p c b -> p b c")).then_inc(st_free, 1)
                v.wait_ge(st_free, g * PAIRS + PAIRS + 2)
                v.wait_ge(sq_free, (g * PAIRS + PAIRS) * 8 + 2)
                ch.start(g * per_group)
                ch.done(nc.vector.tensor_tensor(a1[:, :, :], mu[:, :, :], mu[:, :, :], ALU.mult))
                ch.done(nc.vector.scalar_tensor_tensor(a1[:, :, :], ss[:, :, :], 1.0 / 64, a1[:, :, :], ALU.mult, ALU.subtract))
                ch.done(nc.vector.tensor_scalar(a1[:, :, :], a1[:, :, :], 0.0, 1e-5, ALU.max, ALU.add))
                v.sem_inc(var_ready, 1)
                v.wait_ge(std_ready, g + 1)
                ch.done(nc.vector.reciprocal(a2[:, :, :], a2[:, :, :]))
                ch.done(nc.vector.tensor_tensor(sc[:, :, :], dot[:, :, :], a2[:, :, :], ALU.mult))
                ch.done(nc.vector.tensor_scalar(sc[:, :, :], sc[:, :, :], t["bias_s"][:, :], None, ALU.add))
                ch.done(nc.vector.memset(lo[:, :], 0.0))
                ch.done(nc.vector.tensor_scalar(hi[:, :], lo[:, :], t["bias_s"][:, :], t["bound"][:, :], ALU.add, ALU.add))
                ch.done(nc.vector.tensor_scalar(lo[:, :], lo[:, :], t["bias_s"][:, :], t["bound"][:, :], ALU.add, ALU.subtract))
                first = g * per_group + 9
                v.sem_inc(pace, 1)
                with v.Fori(0, ITER) as i:
                    ch.start(first + i * K_ITER)
                    ch.done(nc.vector.tensor_tensor(mid[:, :], lo[:, :], hi[:, :], ALU.add))
                    ch.done(nc.vector.tensor_scalar(mid[:, :], mid[:, :], 0.5, None, ALU.mult))
                    ch.done(nc.vector.tensor_tensor(a1[:, :, :], sc[:, :, :], bc(mid[:, :], 2, 32), ALU.is_ge))
                    nc.vector.tensor_reduce(cnt[:, :], a1[:, :, :], AX, ALU.add).then_inc(cnt_ready, 1)
                    v.wait_ge(cnt_out, g * SUMS + i + 1)
                    nc.vector.tensor_scalar(geq[:, :], cp[:, :], 2047.5, None, ALU.is_gt)
                    ch.done(nc.vector.tensor_scalar(lss[:, :], cp[:, :], 2047.5, None, ALU.is_lt), pace)
                    ch.done(nc.vector.copy_predicated(lo[:, :], geq[:, :], mid[:, :]), pace)
                    ch.done(nc.vector.copy_predicated(hi[:, :], lss[:, :], mid[:, :]))
                ch.start(first + ITER * K_ITER)
                ch.done(nc.vector.tensor_tensor(sel[:, :, :], sc[:, :, :], bc(hi[:, :], 2, 32), ALU.is_ge))
                ch.done(nc.vector.tensor_tensor(tie[:, :, :], sc[:, :, :], bc(lo[:, :], 2, 32), ALU.is_ge))
                ch.done(nc.vector.tensor_tensor(tie[:, :, :], tie[:, :, :], sel[:, :, :], ALU.subtract))
                nc.vector.tensor_reduce(cnt[:, :], sel[:, :, :], AX, ALU.add).then_inc(cnt_ready, 1)
                v.wait_ge(cnt_out, g * SUMS + ITER + 1)
                ch.done(nc.vector.tensor_scalar(need[:, :], cp[:, :], -1.0, 2048.0, ALU.mult, ALU.add))

                def running(out, of, k):
                    flat = lambda a: a[:, :, :].rearrange("p b c -> p (b c)")
                    ch.done(nc.vector.tensor_tensor_scan(flat(out), flat(t["reset"]), flat(of), 0.0, ALU.mult, ALU.add))
                    nc.vector.tensor_copy(tot[:, :], out[:, :, 31]).then_inc(cnt_ready, 1)
                    v.wait_ge(cnt_out, g * SUMS + ITER + 2 + k)
                    ch.done(nc.vector.tensor_tensor(out[:, :, :], out[:, :, :], of[:, :, :], ALU.subtract))
                    ch.done(nc.vector.tensor_copy(cnt[:, :], cp[:, :]))
                    ch.done(nc.vector.tensor_tensor(out[:, :, :], out[:, :, :], bc(cnt[:, :], 2, 32), ALU.add))

                running(run, tie, 0)
                ch.done(nc.vector.tensor_tensor(a1[:, :, :], run[:, :, :], bc(need[:, :], 2, 32), ALU.is_lt))
                ch.done(nc.vector.tensor_tensor(a1[:, :, :], a1[:, :, :], tie[:, :, :], ALU.mult))
                ch.done(nc.vector.tensor_tensor(sel[:, :, :], sel[:, :, :], a1[:, :, :], ALU.add))
                running(run, sel, 1)
                ch.done(nc.vector.tensor_tensor(run[:, :, :], run[:, :, :],
                                                bc(t["rowbase"][:, bass.ds(g * 8, 8)], 2, 32), ALU.add))
                ch.done(nc.vector.tensor_scalar(run[:, :, :], run[:, :, :], -131072.0, None, ALU.add))
                ch.done(nc.vector.tensor_tensor(run[:, :, :], run[:, :, :], sel[:, :, :], ALU.mult))
                ch.done(nc.vector.tensor_scalar(run[:, :, :], run[:, :, :], 131072.0, None, ALU.add))
                v.wait_ge(sent[gb], g2 * 4096)
                ch.done(nc.vector.tensor_copy(idx[gb][:, :], run[:, :, :].rearrange("p b c -> p (b c)")))
                v.sem_inc(idx_ready, 1)
                assert ch.n + 9 == K_REST, ch.n + 9

        @block.gpsimd
        def _(pool):
            for g2, gb, g in groups(pool):
                pool.wait_ge(idx_ready, g + 1)
                pool.sem_inc(pace_pool, 1)
                for b in range(8):
                    for c in range(32):
                        pool.indirect_dma_start(
                            out=dram["kept"], out_offset=bass.IndirectOffsetOnAxis(ap=idx[gb][:, b * 32 + c:b * 32 + c + 1], axis=0),
                            in_=T[gb][:, b, c, :], in_offset=None, bounds_check=65535, oob_is_err=False).then_inc(sent[gb], 16)
            for gb in range(2):
                pool.wait_ge(sent[gb], 8192)


def attend(nc, t, dram):
    NB, NC, NG = 8, 16, 4
    PER = NB * NC
    kept = dram["kept"].rearrange("(b c p) d -> b p c d", p=128, c=NC)
    h2_rows = dram["h2"]
    node_own = dram["node_own"]
    node_rows = dram["node"].rearrange("(b c p) d -> b p c d", p=128, c=NC)
    with ExitStack() as ctx:
        sem = lambda n: ctx.enter_context(nc.semaphore(n))
        sb = lambda n, s, d=F32: ctx.enter_context(nc.sbuf_tensor(n, s, d))
        pt = lambda n, s: ctx.enter_context(nc.psum_tensor(n, s, F32))
        toep = sb("toep", [128, 64, 128])
        shared = sb("prev_and_xT", [128, 64 * 64])
        toep_prev = shared[:, :].rearrange("p (d m) -> p d m", m=64)
        xT = [shared[0:64, i * 2048:i * 2048 + 2048].rearrange("d (c p) -> d c p", p=128) for i in range(2)]
        H = [sb(f"H{i}", [128, NB, NC, 64]) for i in range(2)]
        Z = sb("Z", [128, NB, NC, 128])
        sq = sb("sq", [128, NC, 64])
        s1, s2, mean, rs, tmp = (sb(n, [128, NB, NC]) for n in ("s1", "s2", "mean", "rs", "lntmp"))
        zb = sb("zb", [128, NB])
        zt = [sb(f"zt{i}", [128, 4, 128]) for i in range(2)]
        y2 = sb("y2", [128, NC, 64])
        nrow = [sb(f"nrow{i}", [128, NC, 28]) for i in range(2)]
        t1, t2, t3, t4 = (sb(n, [128, NC]) for n in ("t1", "t2", "t3", "t4"))
        cps = [pt(f"cps{i}", [128, 4, NB, NC]) for i in range(2)]
        zp = [pt(f"zp{i}", [128, 4, 128]) for i in range(2)]
        op = [pt(f"op{i}", [128, 4, 64]) for i in range(2)]
        xp = pt("xp", [64, 4, 128])
        gp = pt("gp", [128, 512])
        tot_ps = gp[:, 448:448 + NB]
        node_ps = gp[:, 0:448].rearrange("p (c v) -> p c v", v=28)
        toep_in = sem("toep_in")
        h_in = [[sem(f"h_in{i}_{b}") for b in range(2)] for i in range(2)]
        h2_out = [sem("h2_out0"), sem("h2_out1")]
        x_out = [sem("x_out0"), sem("x_out1")]
        node_out = [sem("node_out0"), sem("node_out1")]
        (h_free, sq1, sq1_used, var1, std1, y_ready, tot_ready, zb_ready, conv_ready, conv_out, filt_ready,
         z_ready, zt_ready, o_ready, o_out, h2_ready, sq2, var2, std2, y2_ready, y2_used, xp_ready, xp_out,
         gp_ready, gp_out, dve, pace, z_free) = (sem(n) for n in (
         "h_free", "sq1", "sq1_used", "var1", "std1", "y_ready", "tot_ready", "zb_ready", "conv_ready",
         "conv_out", "filt_ready", "z_ready", "zt_ready", "o_ready", "o_out", "h2_ready", "sq2", "var2", "std2",
         "y2_ready", "y2_used", "xp_ready", "xp_out", "gp_ready", "gp_out", "at_dve", "at_pace", "z_free"))
        block = ctx.enter_context(nc.Block())
        lag = dram["lag_rows"]

        @block.sync
        def _(sp):
            skew = 64 * LAG_W - 1
            sp.dma_start(toep[:, :, :], bass.AP(lag.tensor, 127, [[skew, 128], [LAG_W, 64], [1, 128]])).then_inc(toep_in, 16)
            sp.dma_start(toep_prev[64:128, :, :],
                         bass.AP(lag.tensor, 255 + 64 * skew, [[skew, 64], [LAG_W, 64], [1, 64]])).then_inc(toep_in, 16)
            with sp.Fori(0, 2) as g2:
                for gb in range(2):
                    g = g2 * 2 + gb
                    sp.wait_ge(h_free, g + 1)
                    for half in range(2):
                        b0 = half * 4
                        for b in range(4):
                            sp.dma_start(H[gb][:, b0 + b, :, :], kept[bass.ds(g * NB + b0 + b, 1)].rearrange("a p c d -> (a p) c d")
                                         ).then_inc(h_in[gb][half], 16)

        @block.tensor
        def _(pe):
            pe.wait_ge(toep_in, 32)
            pe.sem_inc(z_free, 1)
            with pe.Fori(0, NG) as g:
                pe.wait_ge(y_ready, g + 1)
                for b in range(NB):
                    for c in range(NC):
                        last = nc.tensor.matmul(tot_ps[64:128, b:b + 1], Z[:, b, c, 0:64], t["ones"][:, 0:1],
                                                start=(c == 0), stop=(c == NC - 1))
                last.then_inc(tot_ready, 1)
                for d4 in range(16):
                    pe.wait_ge(conv_out, g * 16 + d4 + 1)
                    for k in range(4):
                        d = d4 * 4 + k
                        nc.tensor.matmul(cps[d4 % 2][:, k, :, :], toep[:, d, :], Z[:, :, :, d], start=True, stop=True)
                        last = nc.tensor.matmul(cps[d4 % 2][0:64, k, :, 1:NC], toep_prev[64:128, d, :],
                                                Z[64:128, :, 0:NC - 1, d], start=False, stop=True, skip_group_check=True)
                    last.then_inc(conv_ready, 1)
                pe.wait_ge(filt_ready, g * 16 + 16)
                for b in range(NB):
                    n = g * NB + b

                    def turn(c4):
                        pe.wait_ge(zt_ready, n * 4 + c4 - 1 + 2)
                        for j in range(4):
                            last = nc.tensor.transpose(zp[c4 % 2][:, j, :], Z[:, b, c4 * 4 + j, :], t["ident"][:, :])
                        last.then_inc(z_ready, 1)

                    def product(c4):
                        pe.wait_ge(zt_ready, n * 4 + c4 + 1 + 2)
                        pe.wait_ge(o_out, n * 4 + c4 + 1)
                        nc.tensor.matmul(op[c4 % 2][:, :, :].rearrange("p c d -> p (c d)"), t["ones"][0:1, :], t["bias4"][:, :],
                                         start=True, stop=False)
                        for j in range(4):
                            last = nc.tensor.matmul(op[c4 % 2][:, j, :], zt[c4 % 2][:, j, :], t["w12"][:, :],
                                                    start=False, stop=(j == 3))
                        last.then_inc(o_ready, 1)

                    turn(0)
                    for c4 in range(1, 4):
                        turn(c4)
                        product(c4 - 1)
                    product(3)
                    if b == NB - 1:
                        pe.wait_ge(z_ready, n * 4 + 4)
                        pe.sem_inc(z_free, 1)
                    pe.wait_ge(y2_ready, n + 1)
                    for c4 in range(4):
                        pe.wait_ge(xp_out, n * 4 + c4 + 1)
                        pe.sem_inc(pace, 1)
                        for j in range(4):
                            last = nc.tensor.transpose(xp[:, j, :], y2[:, c4 * 4 + j, :], t["ident"][:, :])
                        last.then_inc(xp_ready, 1)
                    pe.wait_ge(xp_out, n * 4 + 5)
                    pe.wait_ge(gp_out, n + 1)
                    for c in range(NC):
                        last = nc.tensor.matmul(node_ps[:, c, :], xT[b % 2][:, c, :], t["w_cat"][:, :], start=True, stop=True)
                    last.then_inc(gp_ready, 1)

        @block.scalar
        def _(act):
            act.sem_inc(conv_out, 2)
            act.sem_inc(zt_ready, 2)
            act.sem_inc(xp_out, 1)
            with act.Fori(0, 2) as g2:
              for gb in range(2):
                g = g2 * 2 + gb
                for b in range(NB):
                    if b % 4 == 0:
                        act.wait_ge(h_in[gb][b // 4], (g2 + 1) * 64)
                    act.wait_ge(sq1_used, g * NB + b + 1)
                    act.activation(sq[:, :, :], H[gb][:, b, :, :], ACT.Square).then_inc(sq1, 1)
                act.wait_ge(var1, g + 1)
                act.activation(rs[:, :, :], tmp[:, :, :], ACT.Sqrt).then_inc(std1, 1)
                for d4 in range(16):
                    act.wait_ge(conv_ready, g * 16 + d4 + 1)
                    act.activation(Z[:, :, :, 64 + d4 * 4:68 + d4 * 4],
                                   cps[d4 % 2][:, :, :, :].rearrange("p k b c -> p b c k"), ACT.Copy).then_inc(filt_ready, 1)
                    act.wait_ge(filt_ready, g * 16 + d4 + 1)
                    act.sem_inc(conv_out, 1)
                act.wait_ge(zb_ready, g + 1)
                for b in range(NB):
                    n = g * NB + b
                    for c4 in range(4):
                        act.wait_ge(z_ready, n * 4 + c4 + 1)
                        act.wait_ge(o_ready, n * 4 + c4 - 2 + 1) if (c4 >= 2) else act.wait_ge(o_ready, n * 4)
                        act.activation(zt[c4 % 2][:, :, :], zp[c4 % 2][:, :, :], ACT.Identity, bias=zb[:, b:b + 1]).then_inc(zt_ready, 1)
                    act.wait_ge(h2_ready, n + 1)
                    act.wait_ge(sq1_used, (g + 1) * NB + 1)
                    act.activation(sq[:, :, :], H[gb][:, b, :, :], ACT.Square).then_inc(sq2, 1)
                    act.wait_ge(var2, n + 1)
                    act.activation(t4[:, :], t3[:, :], ACT.Sqrt).then_inc(std2, 1)
                    act.wait_ge(x_out[b % 2], (g * 4 + b // 2) * 16)
                    act.wait_ge(gp_ready, n)
                    for c4 in range(4):
                        act.wait_ge(xp_ready, n * 4 + c4 + 1)
                        act.activation(xT[b % 2][:, c4 * 4:c4 * 4 + 4, :], xp[:, :, :], ACT.Copy).then_inc(xp_out, 1)
                    act.wait_ge(xp_out, n * 4 + 5)
                    act.dma_start(dram["x3t"].rearrange("d (n t) -> d n t", t=2048)[:, bass.ds(n, 1), :].rearrange("d a t -> d (a t)"),
                                  shared[0:64, b % 2 * 2048:b % 2 * 2048 + 2048]).then_inc(x_out[b % 2], 16)

        @block.vector
        def _(v):
            v.sem_inc(sq1_used, 1)
            v.sem_inc(o_out, 2)
            v.sem_inc(gp_out, 1)
            ch = Chain(v, dve)
            K = 86
            nc.vector.memset(zb[0:64, :], 0.0)
            with v.Fori(0, 2) as g2:
              for gb in range(2):
                g = g2 * 2 + gb
                ch.start(g * K)
                for b in range(NB):
                    if b % 4 == 0:
                        v.wait_ge(h_in[gb][b // 4], (g2 + 1) * 64)
                    nc.vector.tensor_reduce(s1[:, b, :], H[gb][:, b, :, :], AX, ALU.add)
                    v.wait_ge(sq1, g * NB + b + 1)
                    nc.vector.tensor_reduce(s2[:, b, :], sq[:, :, :], AX, ALU.add).then_inc(sq1_used, 1)
                v.wait_ge(sq1_used, (g + 1) * NB + 1)
                ch.done(nc.vector.tensor_scalar(mean[:, :, :], s1[:, :, :], 1.0 / 64, None, ALU.mult))
                ch.done(nc.vector.tensor_tensor(tmp[:, :, :], mean[:, :, :], mean[:, :, :], ALU.mult))
                ch.done(nc.vector.scalar_tensor_tensor(tmp[:, :, :], s2[:, :, :], 1.0 / 64, tmp[:, :, :], ALU.mult, ALU.subtract))
                ch.done(nc.vector.tensor_scalar(tmp[:, :, :], tmp[:, :, :], 0.0, 1e-5, ALU.max, ALU.add))
                v.sem_inc(var1, 1)
                v.wait_ge(std1, g + 1)
                ch.done(nc.vector.reciprocal(rs[:, :, :], rs[:, :, :]))
                v.wait_ge(z_free, g + 1)
                for b in range(NB):
                    nc.vector.tensor_tensor(Z[:, b, :, 0:64], H[gb][:, b, :, :], bc(mean[:, b, :], 2, 64), ALU.subtract).then_inc(dve, 1)
                    ch.n += 1
                    if b:
                        v.wait_ge(dve, ch.base + ch.n - 1)
                        nc.vector.tensor_tensor(Z[:, b - 1, :, 0:64], Z[:, b - 1, :, 0:64], bc(rs[:, b - 1, :], 2, 64), ALU.mult)
                ch.done(nc.vector.tensor_scalar(t1[:, :], t["reset"][:, 0, 0:16], 0.0, None, ALU.mult))
                nc.vector.tensor_tensor(Z[:, 7, :, 0:64], Z[:, 7, :, 0:64], bc(rs[:, 7, :], 2, 64), ALU.mult).then_inc(y_ready, 1)
                v.wait_ge(tot_ready, g + 1)
                nc.vector.tensor_scalar(zb[64:128, :], tot_ps[64:128, :], t["m0"][64:128, :], None, ALU.mult).then_inc(zb_ready, 1)
                for b in range(NB):
                    n = g * NB + b
                    for c4 in range(4):
                        v.wait_ge(o_ready, n * 4 + c4 + 1)
                        nc.vector.tensor_tensor(H[gb][:, b, c4 * 4:c4 * 4 + 4, :], op[c4 % 2][:, :, :],
                                                H[gb][:, b, c4 * 4:c4 * 4 + 4, :], ALU.add).then_inc(o_out, 1)
                    v.wait_ge(o_out, n * 4 + 6)
                    v.sem_inc(h2_ready, 1)
                    hh = H[gb][:, b, :, :]
                    ch.done(nc.vector.tensor_reduce(t1[:, :], hh, AX, ALU.add))
                    ch.done(nc.vector.tensor_scalar(t1[:, :], t1[:, :], 1.0 / 64, None, ALU.mult))
                    ch.done(nc.vector.tensor_tensor(t2[:, :], t1[:, :], t1[:, :], ALU.mult))
                    v.wait_ge(sq2, n + 1)
                    ch.done(nc.vector.tensor_reduce(t3[:, :], sq[:, :, :], AX, ALU.add))
                    ch.done(nc.vector.scalar_tensor_tensor(t3[:, :], t3[:, :], 1.0 / 64, t2[:, :], ALU.mult, ALU.subtract))
                    ch.done(nc.vector.tensor_scalar(t3[:, :], t3[:, :], 0.0, 1e-5, ALU.max, ALU.add))
                    v.sem_inc(var2, 1)
                    v.wait_ge(xp_ready, n * 4)
                    ch.done(nc.vector.tensor_tensor(y2[:, :, :], hh, bc(t1[:, :], 2, 64), ALU.subtract))
                    v.wait_ge(std2, n + 1)
                    ch.done(nc.vector.reciprocal(t4[:, :], t4[:, :]))
                    nc.vector.tensor_tensor(y2[:, :, :], y2[:, :, :], bc(t4[:, :], 2, 64), ALU.mult).then_inc(y2_ready, 1)
                    v.wait_ge(y2_ready, n + 1)
                    v.wait_ge(node_out[b % 2], (g * 4 + b // 2) * 32)
                    v.wait_ge(gp_ready, n + 1)
                    ch.done(nc.vector.tensor_tensor(nrow[b % 2][:, :, :], node_ps, bc(t["unit"][:, :], 1, NC), ALU.add))
                    v.sem_inc(gp_out, 1)
                ch_n = ch.n
            assert ch_n == K, ch_n

        @block.gpsimd
        def _(pool):
            pool.sem_inc(h_free, 2)
            with pool.Fori(0, NG // 2) as g2:
                for gb in range(2):
                    g = g2 * 2 + gb
                    for b in range(NB):
                        n, s = g * NB + b, b % 2
                        pool.wait_ge(h2_ready, n + 1)
                        pool.dma_start(h2_rows[bass.ds(n, 1)].rearrange("a p c d -> (a p) c d"), H[gb][:, b, :, :]).then_inc(h2_out[s], 16)
                        pool.wait_ge(gp_out, n + 2)
                        pool.dma_start(node_rows[bass.ds(n, 1)].rearrange("a p c d -> (a p) c d"), nrow[s][:, :, :]).then_inc(node_out[s], 16)
                        pool.dma_start(node_own[bass.ds(n, 1)].rearrange("a p c d -> (a p) c d"), nrow[s][:, :, :]).then_inc(node_out[s], 16)
                    for s in range(2):
                        pool.wait_ge(h2_out[s], (g + 1) * 64)
                    pool.sem_inc(h_free, 1)
            for s in range(2):
                pool.wait_ge(h2_out[s], 256)
                pool.wait_ge(node_out[s], 512)
                pool.wait_ge(x_out[s], 256)


def phase_stages():
    step = 0
    for k in range(1, 19):
        for j in range(k - 1, -1, -1):
            yield step, k, j
            step += 1


def crossings():
    return [step for step, k, j in phase_stages() if k > 11 and j in (k - 1, 10)]


def sort_edges(nc, t, dram):
    with ExitStack() as ctx:
        sem = lambda n: ctx.enter_context(nc.semaphore(n))
        sb = lambda n, s, d=U16: ctx.enter_context(nc.sbuf_tensor(n, s, d))
        key = [sb(f"key{i}", [128, COLS]) for i in range(2)]
        src = sb("src", [128, COLS])
        raw = [sb(f"raw{i}", [128, COLS], I32) for i in range(2)]
        swapped, delta = sb("swapped", [128, COLS // 2]), sb("delta", [128, COLS // 2])
        pid, bit = sb("pid", [128, 8], I32), sb("bit", [128, 8], F32)
        sign, off = sb("sign", [128, 9], F32), sb("off", [128, 9], F32)
        edges_in, dve, left, back, turned, pid_ready = (sem(n) for n in
            ("edges_in", "sort_dve", "left", "back", "turned", "pid_ready"))
        cross = crossings()
        scratch = dram["sort_scratch"]
        block = ctx.enter_context(nc.Block())

        @block.gpsimd
        def _(pool):
            nc.gpsimd.iota(pid[:, :], pattern=[[0, 8]], base=0, channel_multiplier=1).then_inc(pid_ready, 1)

        @block.sync
        def _(sp):
            e = dram["edges"].rearrange("k (p f) -> k p f", p=128)
            sp.dma_start(raw[0][:, :], e[0]).then_inc(edges_in, 16)
            sp.dma_start(raw[1][:, :], e[1]).then_inc(edges_in, 16)
            for n, step in enumerate(cross):
                sp.wait_ge(turned, n + 1)
                sp.dma_start(scratch[0], key[step % 2][:, :]).then_inc(left, 16)
                sp.dma_start(scratch[1], src[:, :]).then_inc(left, 16)
                sp.wait_ge(left, 32 * (n + 1))
                for k, dst in enumerate((key[step % 2], src)):
                    sp.dma_start(dst[:, :].rearrange("q (p l) -> q p l", l=16),
                                 scratch[k].rearrange("p (q l) -> q p l", l=16)).then_inc(back, 16)
            sp.wait_ge(turned, len(cross) + 1)
            sp.dma_start(dram["sorted_dst"], key[171 % 2][:, :]).then_inc(left, 16)
            sp.dma_start(dram["sorted_src"], src[:, :]).then_inc(left, 16)
            sp.wait_ge(left, 32 * (len(cross) + 1))

        @block.vector
        def _(v):
            ch = Chain(v, dve)
            v.wait_ge(edges_in, 32)
            ch.done(nc.vector.tensor_copy(src[:, :], raw[0][:, :]))
            ch.done(nc.vector.tensor_copy(key[0][:, :], raw[1][:, :]))
            v.wait_ge(pid_ready, 1)
            for r in range(7):
                ch.done(nc.vector.tensor_scalar(pid[:, r:r + 1], pid[:, r:r + 1], r, 1,
                                                ALU.logical_shift_right, ALU.bitwise_and))
            ch.done(nc.vector.tensor_copy(bit[:, 0:7], pid[:, 0:7]))
            ch.done(nc.vector.tensor_copy(sign[:, 0:1], bit[:, 0:1]))
            ch.done(nc.vector.tensor_scalar(sign[:, 1:2], bit[:, 0:1], -1.0, 1.0, ALU.mult, ALU.add))
            ch.done(nc.vector.tensor_tensor(sign[:, 2:8], bit[:, 0:6], bit[:, 1:7], ALU.not_equal))
            ch.done(nc.vector.tensor_copy(sign[:, 8:9], bit[:, 6:7]))
            ch.done(nc.vector.tensor_scalar(off[:, :], sign[:, :], 65535.0, None, ALU.mult))
            ch.done(nc.vector.tensor_scalar(sign[:, :], sign[:, :], -2.0, 1.0, ALU.mult, ALU.add))

            def complement(part, column=None):
                if column is None:
                    ch.done(nc.vector.tensor_scalar(part, part, -1.0, 65535.0, ALU.mult, ALU.add))
                else:
                    ch.done(nc.vector.tensor_scalar(part, part, sign[:, column:column + 1], off[:, column:column + 1],
                                                    ALU.mult, ALU.add))

            def halves(tile, d):
                pairs = tile[:, :].rearrange("p (n t d) -> p n t d", t=2, d=d)
                return pairs[:, :, 0, :], pairs[:, :, 1, :]

            complement(key[0][:, :].rearrange("p (n f) -> p n f", f=4)[:, :, 2:4])
            for step, k, j in phase_stages():
                if step in cross:
                    v.sem_inc(turned, 1)
                    v.wait_ge(back, 32 * (cross.index(step) + 1))
                d = 1 << (j - 7 if j > 10 else j)
                a, b = halves(key[step % 2], d)
                low, high = halves(key[1 - step % 2], d)
                src_a, src_b = halves(src, d)
                m, x = (q[:, :].rearrange("p (n d) -> p n d", d=d) for q in (swapped, delta))
                nc.vector.tensor_tensor(m, a, b, ALU.is_gt)
                ch.done(nc.vector.tensor_tensor(x, src_a, src_b, ALU.bitwise_xor))
                nc.vector.tensor_tensor(low, a, b, ALU.min)
                ch.done(nc.vector.tensor_tensor(x, x, m, ALU.mult))
                nc.vector.tensor_tensor(high, a, b, ALU.max)
                nc.vector.tensor_tensor(src_a, src_a, x, ALU.bitwise_xor)
                ch.done(nc.vector.tensor_tensor(src_b, src_b, x, ALU.bitwise_xor))
                if j == 0:
                    done = key[1 - step % 2]
                    if k < 10:
                        complement(done[:, :].rearrange("p (n f) -> p n f", f=4 << k)[:, :, 1 << k:3 << k])
                    elif k == 10:
                        complement(done[:, 0:1024], 0)
                        complement(done[:, 1024:2048], 1)
                    elif k < 18:
                        complement(done[:, :], k - 9)
            v.sem_inc(turned, 1)


def count_edges(nc, t, dram):
    with ExitStack() as ctx:
        sem = lambda n: ctx.enter_context(nc.semaphore(n))
        sb = lambda n, s, d=F32: ctx.enter_context(nc.sbuf_tensor(n, s, d))
        pt = lambda n, s: ctx.enter_context(nc.psum_tensor(n, s, F32))
        SLOTS = 4
        dst = sb("c_dst", [128, COLS], U16)
        lo16, hi16 = sb("lo16", [128, COLS], U16), sb("hi16", [128, COLS], U16)
        lo, hi = sb("c_lo", [128, COLS]), sb("c_hi", [128, COLS])
        num_i, num = sb("num_i", [128, 512], I32), sb("num", [128, 512], U16)
        is_lo = [sb(f"is_lo{i}", [128, 128], BF16) for i in range(SLOTS)]
        is_hi = [sb(f"is_hi{i}", [128, 512], BF16) for i in range(SLOTS)]
        count, start, end, none = (sb(n, [128, 512]) for n in ("count", "start", "end", "none"))
        busy_f = sb("busy_f", [1, NODE_TILES // SKIP_GROUP])
        cps, tps, bps = pt("count_ps", [128, 512]), pt("total_ps", [128, 512]), pt("before_ps", [128, 512])
        dst_in, num_ready, hot, hot_free, counted, summed, dve, count_ready = (sem(n) for n in
            ("dst_in", "num_ready", "hot", "hot_free", "counted", "summed", "count_dve", "count_ready"))
        block = ctx.enter_context(nc.Block())

        @block.sync
        def _(sp):
            sp.dma_start(dst[:, :], dram["sorted_dst"]).then_inc(dst_in, 16)

        @block.gpsimd
        def _(pool):
            nc.gpsimd.iota(num_i[:, :], pattern=[[1, 512]], base=0, channel_multiplier=0).then_inc(num_ready, 1)

        @block.vector
        def _(v):
            ch = Chain(v, dve)
            v.wait_ge(dst_in, 16)
            v.wait_ge(num_ready, 1)
            ch.done(nc.vector.tensor_copy(num[:, :], num_i[:, :]))
            ch.done(nc.vector.tensor_scalar(lo16[:, :], dst[:, :], 127, None, ALU.bitwise_and))
            ch.done(nc.vector.tensor_scalar(hi16[:, :], dst[:, :], 7, None, ALU.logical_shift_right))
            ch.done(nc.vector.tensor_copy(lo[:, :], lo16[:, :]))
            ch.done(nc.vector.tensor_copy(hi[:, :], hi16[:, :]))
            v.sem_inc(hot_free, SLOTS)
            with v.Fori(0, COLS // SLOTS) as i:
                for s in range(SLOTS):
                    v.wait_ge(hot_free, i * SLOTS + s + 1)
                    nc.vector.tensor_scalar(is_lo[s][:, :], num[:, 0:128], lo[:, bass.ds(i * SLOTS + s, 1)], None, ALU.is_equal)
                    nc.vector.tensor_scalar(is_hi[s][:, :], num[:, :], hi[:, bass.ds(i * SLOTS + s, 1)], None, ALU.is_equal).then_inc(hot, 1)
            v.wait_ge(counted, 1)
            ch.done(nc.vector.tensor_copy(count[:, :], cps[:, :]))
            v.sem_inc(count_ready, 1)
            v.wait_ge(summed, 2)
            ch.done(nc.vector.memset(none[:, :], 1.0))
            ch.done(nc.vector.tensor_copy(end[:, :], tps[:, :]))
            ch.done(nc.vector.tensor_tensor_scan(start[:, :], none[:, :], end[:, :], 0.0, ALU.mult, ALU.add))
            ch.done(nc.vector.tensor_tensor(start[:, :], start[:, :], end[:, :], ALU.subtract))
            ch.done(nc.vector.tensor_reduce(busy_f[:, :], end[0:1, :].rearrange("a (g c) -> a g c", c=SKIP_GROUP), AX, ALU.add))
            ch.done(nc.vector.tensor_copy(t["busy"][:, :], busy_f[:, :]))
            ch.done(nc.vector.tensor_copy(end[:, :], bps[:, :]))
            ch.done(nc.vector.tensor_tensor(start[:, :], start[:, :], end[:, :], ALU.add))
            ch.done(nc.vector.scalar_tensor_tensor(end[:, :], start[:, :], -1.0, count[:, :], ALU.add, ALU.add))
            ch.done(nc.vector.tensor_scalar(none[:, :], count[:, :], 0.5, float(SKIP), ALU.is_lt, ALU.mult))
            ch.done(nc.vector.tensor_tensor(start[:, :], start[:, :], none[:, :], ALU.max))
            ch.done(nc.vector.tensor_tensor(end[:, :], end[:, :], none[:, :], ALU.max))
            ch.done(nc.vector.tensor_copy(t["first_edge"][:, :], start[:, :]))
            ch.done(nc.vector.tensor_copy(t["last_edge"][:, :], end[:, :]))

        @block.tensor
        def _(pe):
            def add(s, start):
                return nc.tensor.matmul(cps[:, :], is_lo[s][:, :], is_hi[s][:, :], start=start, stop=True, skip_group_check=True)

            for s in range(SLOTS):
                pe.wait_ge(hot, s + 1)
                add(s, s == 0).then_inc(hot_free, 1)
            with pe.Fori(1, COLS // SLOTS) as i:
                for s in range(SLOTS):
                    pe.wait_ge(hot, i * SLOTS + s + 1)
                    add(s, False).then_inc(hot_free, 1)
            pe.wait_ge(hot_free, COLS + SLOTS)
            pe.sem_inc(counted, 1)
            pe.wait_ge(count_ready, 1)
            nc.tensor.matmul(tps[:, :], t["ones"][:, :], count[:, :], start=True, stop=True).then_inc(summed, 1)
            nc.tensor.matmul(bps[:, :], t["before"][:, :], count[:, :], start=True, stop=True).then_inc(summed, 1)


CHUNK = 256
CHUNKS = COLS // CHUNK
ROW = 28
SKIP_GROUP = 8


def busy_tiles(pool, t, move, sem, nothing):
    for g in range(NODE_TILES // SKIP_GROUP):
        some = pool.value_load(t["busy"][0:1, g:g + 1])
        with pool.If(some > 0):
            for c in range(g * SKIP_GROUP, (g + 1) * SKIP_GROUP):
                move(c).then_inc(sem, 16)
        with pool.Else():
            pool.dma_start(nothing[g:g + 1, :], t["busy"][0:1, 0:1]).then_inc(sem, 16 * SKIP_GROUP)


def pass_messages(nc, t, dram):
    edge_ad = dram["edge_ad"]
    runs = dram["runs"]
    with ExitStack() as ctx:
        sem = lambda n: ctx.enter_context(nc.semaphore(n))
        sb = lambda n, s, d=F32: ctx.enter_context(nc.sbuf_tensor(n, s, d))
        pt = lambda n, s: ctx.enter_context(nc.psum_tensor(n, s, F32))
        E = [t["edge_rows"][:, i * CHUNK * ROW:(i + 1) * CHUNK * ROW].rearrange("p (f v) -> p f v", v=ROW) for i in range(2)]
        node_run = t["edge_rows"][:, :].rearrange("p (c v) -> p c v", v=ROW)
        dst, src = sb("m_dst", [128, COLS], U16), sb("m_src", [128, COLS + 2 * CHUNK], U16)
        same = sb("same", [128, COLS])
        same_neg = sb("same_neg", [128, CHUNK])
        idx = [sb(f"src_row{i}", [128, CHUNK], I32) for i in range(2)]
        ad = [sb(f"ad{i}", [128, CHUNK, 4]) for i in range(2)]
        node_ad = sb("node_ad", [128, NODE_TILES, 4])
        score = sb("e_score", [128, CHUNK, 4])
        top = sb("top", [128, CHUNK + 1, 4])
        X = sb("X", [128, 2, CHUNK, 4])
        ad_last = sb("ad_last", [128, 4])
        sum_last = sb("sum_last", [128, 20])
        zeros = sb("zeros", [128, 1024])
        border = sb("border", [128, 2], U16)
        first_i = sb("first_i", [128, 2], I32)
        first_row = sb("first_row", [128, ROW])
        tail = sb("tail", [128, ROW])
        chain = sb("chain", [1, 128, ROW])
        chain_top = sb("chain_top", [1, 129, 4])
        chain_x = sb("chain_x", [1, 2, 128, 4])
        ends16 = sb("ends16", [1, 2, 128], U16)
        link = sb("link", [1, 3, 128])
        carry, patch = sb("carry", [128, ROW]), sb("patch", [128, ROW])
        px = sb("px", [128, 3, 4])
        place = sb("place", [128, 4])
        place_i = sb("place_i", [128, 2], I32)
        w1, w2 = sb("w1", [64, 4, 128]), sb("w2", [128, 4, 64])
        b1, b2 = sb("b1", [128, 4]), sb("b2", [128, 4, 64])
        xT = sb("mxT", [64, 2048])
        hid = [sb(f"hid{i}", [128, 512]) for i in range(2)]
        ot = [sb(f"ot{i}", [128, 4, 16, 64]) for i in range(2)]
        hp = [pt(f"hp{i}", [128, 512]) for i in range(2)]
        eo = [pt(f"eo{i}", [128, 4, 64]) for i in range(2)]
        (small_in, dst_in, src_in, zero_ready, zero_out, node_ad_in, first_in, ad_out, gat_free, idx_ready, x_ready,
         exp_ready, rows_ready, h_ready, g_ready, e_ready, eo_out, ot_done, tail_ready, chain_x_ready,
         chain_exp, carry_ready, place_ready, patch_in, patch_ready, patch_out, px_ready, px_exp, init_ready,
         dve, fin, tails_out, chain_in, carry_out, carry_in, first_ready, pace, mx_in, pace_pool) = (sem(n) for n in (
         "m_small_in", "m_dst_in", "m_src_in", "zero_ready", "zero_out", "node_ad_in", "first_in", "ad_out", "gat_free",
         "idx_ready2", "x_ready", "exp_ready", "rows_ready", "h_ready", "g_ready", "e_ready", "eo_out",
         "ot_done", "tail_ready", "chain_x_ready", "chain_exp", "carry_ready", "place_ready", "patch_in",
         "patch_ready", "patch_out", "px_ready", "px_exp", "init_ready", "m_dve", "m_fin", "tails_out", "chain_in",
         "carry_out", "carry_in", "first_ready", "m_pace", "mx_in", "m_pace_pool"))
        gathered = [sem("gathered0"), sem("gathered1")]
        ad_in = [sem("ad_in0"), sem("ad_in1")]
        runs_out = [sem("runs_out0"), sem("runs_out1")]
        ot_out = [sem("ot_out0"), sem("ot_out1")]
        block = ctx.enter_context(nc.Block())
        row = lambda v: v.rearrange("(a n) -> a n", a=1)
        ad_c = edge_ad.rearrange("(p f) v -> p f v", p=128)
        runs_c = runs.rearrange("(p f) v -> p f v", p=128)
        experts = dram["experts"]

        @block.sync
        def _(sp):
            sp.dma_start(dst[:, :], dram["sorted_dst"]).then_inc(dst_in, 16)
            sp.dma_start(border[1:128, 0:1], dram["sorted_dst"][0:127, COLS - 1:COLS], allow_slow_non_contiguous=True).then_inc(dst_in, 16)
            sp.dma_start(src[:, 0:COLS], dram["sorted_src"]).then_inc(src_in, 16)
            sp.wait_ge(zero_ready, 1)
            flat = edge_ad.rearrange("(p f) v -> p (f v)", p=128)
            for k in range(8):
                sp.dma_start(flat[:, k * 1024:(k + 1) * 1024], zeros[:, :]).then_inc(zero_out, 16)
            sp.dma_start(node_ad[:, :, :], dram["node"].rearrange("(c p) v -> p c v", p=128)[:, :, 24:28]).then_inc(node_ad_in, 16)
            sp.dma_start(w1[:, :, :], dram["F_W1"].rearrange("e d f -> d e f")).then_inc(small_in, 16)
            sp.dma_start(w2[:, :, :], dram["F_W2"].rearrange("e f d -> f e d")).then_inc(small_in, 16)
            sp.dma_start(b1[:, :], dram["F_b1"].rearrange("e f -> f e"), allow_slow_non_contiguous=True).then_inc(small_in, 16)
            sp.dma_start(b2[:, :, :].rearrange("p e d -> p (e d)"),
                         row(dram["F_b2"].rearrange("e d -> (e d)")).to_broadcast([128, 256])).then_inc(small_in, 16)
            for k, c in enumerate((0, COLS - 1)):
                sp.dma_start(ends16[:, k, :], dram["sorted_dst"][:, c:c + 1].rearrange("p one -> one p"),
                             allow_slow_non_contiguous=True).then_inc(small_in, 16)
            sp.wait_ge(ad_out, 16 * NODE_TILES)
            with sp.Fori(0, CHUNKS // 2) as k2:
                for s in range(2):
                    k = k2 * 2 + s
                    sp.wait_ge(gat_free, k + 1)
                    sp.dma_start(ad[s][:, :, :], ad_c[:, bass.ds(k * CHUNK, CHUNK), :]).then_inc(ad_in[s], 16)
                    with sp.Fori(0, 2) as m2:
                        for m in range(2):
                            n = k * 4 + m2 * 2 + m
                            sp.wait_ge(ot_done, n + 1)
                            sp.dma_start(experts[bass.ds(n, 1)].rearrange("a p v -> (a p) v"),
                                         ot[m][:, :, :, :].rearrange("p e c d -> p (e c d)")).then_inc(ot_out[m], 16)
                    sp.wait_ge(rows_ready, k + 1)
                    sp.dma_start(runs_c[:, bass.ds(k * CHUNK, CHUNK), :], E[s][:, :, :]).then_inc(runs_out[s], 16)
            sp.wait_ge(tail_ready, 1)
            sp.dma_start(dram["tails"], tail[:, :]).then_inc(tails_out, 16)
            sp.wait_ge(tails_out, 16)
            sp.dma_start(chain[:, :, :].rearrange("a p v -> a (p v)"), row(dram["tails"].rearrange("p v -> (p v)"))).then_inc(chain_in, 16)
            sp.wait_ge(carry_ready, 1)
            sp.dma_start(row(dram["carries"].rearrange("p v -> (p v)")), chain[:, :, :].rearrange("a p v -> a (p v)")).then_inc(carry_out, 16)
            sp.wait_ge(carry_out, 16)
            sp.dma_start(carry[1:128, :], dram["carries"][0:127, :]).then_inc(carry_in, 16)
            for s in range(2):
                sp.wait_ge(ot_out[s], 16 * 16)

        @block.gpsimd
        def _(pool):
            nc.gpsimd.iota(place_i[:, 0:1], pattern=[[0, 1]], base=0, channel_multiplier=COLS).then_inc(place_ready, 1)
            pool.wait_ge(first_ready, 1)
            pool.indirect_dma_start(out=first_row[:, :], out_offset=None, in_=dram["node"],
                                    in_offset=bass.IndirectOffsetOnAxis(ap=first_i[:, 0:1], axis=0)).then_inc(first_in, 16)
            pool.wait_ge(zero_out, 128)
            pool.wait_ge(node_ad_in, 16)
            pool.sem_inc(pace_pool, 1)
            busy_tiles(pool, t, lambda c: pool.indirect_dma_start(
                out=edge_ad, out_offset=bass.IndirectOffsetOnAxis(ap=t["first_edge"][:, c:c + 1], axis=0),
                in_=node_ad[:, c, :], in_offset=None, bounds_check=N_EDGES - 1, oob_is_err=False), ad_out, dram["nothing"][0])
            with pool.Fori(0, CHUNKS // 2) as k2:
                for s in range(2):
                    k = k2 * 2 + s
                    pool.wait_ge(idx_ready, k + 1)
                    pool.wait_ge(runs_out[s], k2 * 16)
                    pool.sem_inc(pace_pool, 1)
                    for f in range(CHUNK):
                        pool.indirect_dma_start(out=E[s][:, f, :], out_offset=None, in_=dram["node"],
                                                in_offset=bass.IndirectOffsetOnAxis(ap=idx[s][:, f:f + 1], axis=0)
                                                ).then_inc(gathered[s], 16)
            pool.wait_ge(place_ready, 3)
            for s in range(2):
                pool.wait_ge(runs_out[s], CHUNKS * 8)
            at = bass.IndirectOffsetOnAxis(ap=place_i[:, 1:2], axis=0)
            pool.indirect_dma_start(out=patch[:, :], out_offset=None, in_=runs, in_offset=at,
                                    bounds_check=N_EDGES - 1, oob_is_err=False).then_inc(patch_in, 16)
            pool.wait_ge(patch_ready, 1)
            pool.indirect_dma_start(out=runs, out_offset=at, in_=patch[:, :], in_offset=None,
                                    bounds_check=N_EDGES - 1, oob_is_err=False).then_inc(patch_out, 16)
            pool.wait_ge(patch_out, 16)
            pool.wait_ge(init_ready, 1)
            busy_tiles(pool, t, lambda c: pool.indirect_dma_start(
                out=node_run[:, c, :], out_offset=None, in_=runs,
                in_offset=bass.IndirectOffsetOnAxis(ap=t["last_edge"][:, c:c + 1], axis=0),
                bounds_check=N_EDGES - 1, oob_is_err=False), fin, dram["nothing"][1])
            pool.wait_ge(fin, 16 * NODE_TILES)

        @block.tensor
        def _(pe):
            pe.wait_ge(small_in, 16 * 6)
            pe.sem_inc(e_ready, 16)
            with pe.Fori(0, 32) as n:
                pe.wait_ge(mx_in, (n + 1) * 16)

                def second(u):
                    pe.wait_ge(g_ready, n * 16 + u + 1)
                    pe.wait_ge(eo_out, n * 16 + u + 1)
                    for j in range(4):
                        last = nc.tensor.matmul(eo[u % 2][:, j, :], hid[u % 2][:, j * 128:(j + 1) * 128], w2[:, u % 4, :],
                                                start=True, stop=True)
                    last.then_inc(e_ready, 1)

                for u in range(16):
                    pe.wait_ge(g_ready, n * 16 + max(u - 1, 0))
                    nc.tensor.matmul(hp[u % 2][:, :], w1[:, u % 4, :], xT[:, (u // 4) * 512:(u // 4) * 512 + 512],
                                     start=True, stop=True).then_inc(h_ready, 1)
                    if u:
                        second(u - 1)
                second(15)

        @block.scalar
        def _(act):
            with act.Fori(0, CHUNKS) as k:
                with act.Fori(0, 4) as m:
                    n = k * 4 + m
                    act.dma_start(xT[:, :], dram["x3t"].rearrange("d (n t) -> d n t", t=2048)[:, bass.ds(n, 1), :]
                                  .rearrange("d a t -> d (a t)")).then_inc(mx_in, 16)
                    for u in range(16):
                        act.wait_ge(h_ready, n * 16 + u + 1)
                        act.wait_ge(e_ready, n * 16 + u + 15)
                        act.activation(hid[u % 2][:, :], hp[u % 2][:, :], ACT.Gelu, bias=b1[:, u % 4:u % 4 + 1]).then_inc(g_ready, 1)
                act.wait_ge(x_ready, k + 1)
                act.activation(X[:, :, :, :], X[:, :, :, :], ACT.Exp).then_inc(exp_ready, 1)
            act.wait_ge(chain_x_ready, 1)
            act.activation(chain_x[:, :, :, :], chain_x[:, :, :, :], ACT.Exp).then_inc(chain_exp, 1)
            act.wait_ge(px_ready, 1)
            act.activation(px[:, 1:3, :], px[:, 1:3, :], ACT.Exp).then_inc(px_exp, 1)

        @block.vector
        def _(v):
            ch = Chain(v, dve)
            v.sem_inc(gat_free, 2)
            v.sem_inc(eo_out, 2)
            nc.vector.memset(zeros[:, :], 0.0).then_inc(zero_ready, 1)
            ch.done(nc.vector.memset(sum_last[:, :], 0.0))
            ch.done(nc.vector.memset(top[:, 0:1, :], LOW))
            ch.done(nc.vector.memset(tail[:, :], 0.0))
            ch.done(nc.vector.memset(carry[:, :], 0.0))
            ch.done(nc.vector.memset(patch[:, :], 0.0))
            ch.done(nc.vector.memset(place[:, :], 0.0))
            ch.done(nc.vector.memset(src[:, COLS:], 0))
            ch.done(nc.vector.memset(border[0:1, 0:1], 0))
            v.wait_ge(dst_in, 32)
            ch.done(nc.vector.tensor_copy(first_i[:, 0:1], dst[:, 0:1]))
            v.sem_inc(first_ready, 1)
            nc.vector.tensor_tensor(same[:, 1:COLS], dst[:, 1:COLS], dst[:, 0:COLS - 1], ALU.is_equal)
            ch.done(nc.vector.tensor_tensor(same[:, 0:1], dst[:, 0:1], border[:, 0:1], ALU.is_equal))
            ch.done(nc.vector.memset(same[0:1, 0:1], 0.0))
            v.wait_ge(first_in, 16)
            ch.done(nc.vector.tensor_copy(ad_last[:, :], first_row[:, 24:28]))
            v.wait_ge(src_in, 16)
            ch.done(nc.vector.tensor_copy(idx[0][:, :], src[:, 0:CHUNK]))
            v.sem_inc(idx_ready, 1)
            ch.done(nc.vector.tensor_copy(idx[1][:, :], src[:, CHUNK:2 * CHUNK]))
            v.sem_inc(idx_ready, 1)
            v.wait_ge(small_in, 96)
            base = ch.n

            def segment_run(rows, high, score_t, neg_t, x, sum_before, asked, answered, answers):
                F = rows.shape[1]
                now, before = high[:, 1:F + 1, :], high[:, 0:F, :]
                for h in range(4):
                    last = nc.vector.tensor_tensor_scan(high[:, 1:F + 1, h], neg_t, score_t[:, :, h], high[:, 0:1, h],
                                                        ALU.add, ALU.max)
                ch.done(last)
                nc.vector.tensor_tensor(x[:, 1, :, :], score_t, now, ALU.subtract)
                ch.done(nc.vector.tensor_tensor(x[:, 0, :, :], before, bc(neg_t, 2, 4), ALU.add))
                ch.done(nc.vector.tensor_tensor(x[:, 0, :, :], x[:, 0, :, :], now, ALU.subtract))
                v.sem_inc(asked, 1)
                v.wait_ge(answered, answers)
                sums = rows[:, :, 0:20].rearrange("p f (h v) -> p f h v", v=5)
                ch.done(nc.vector.tensor_tensor(sums, sums, bc(x[:, 1, :, :], 3, 5), ALU.mult))
                for c in range(20):
                    last = nc.vector.tensor_tensor_scan(rows[:, :, c], x[:, 0, :, c // 5], rows[:, :, c], sum_before(c), ALU.mult, ALU.add)
                ch.done(last)
                ch.done(nc.vector.tensor_copy(rows[:, :, 20:24], now))

            K = 13
            with v.Fori(0, CHUNKS // 2) as k2:
                for s in range(2):
                    k = k2 * 2 + s
                    with v.Fori(0, 2) as m2:
                        for m in range(2):
                            n = k * 4 + m2 * 2 + m
                            v.wait_ge(ot_out[m], (k * 2 + m2) * 16)
                            for u in range(16):
                                v.wait_ge(e_ready, n * 16 + u + 17)
                                c0 = u // 4 * 4
                                nc.vector.tensor_tensor(ot[m][:, u % 4, c0:c0 + 4, :], eo[u % 2][:, :, :],
                                                        bc(b2[:, u % 4, :], 1, 4), ALU.add).then_inc(eo_out, 1)
                            v.wait_ge(eo_out, n * 16 + 18)
                            v.sem_inc(ot_done, 1)
                    ch.start(base + k * K)
                    v.wait_ge(ad_in[s], (k2 + 1) * 16)
                    v.sem_inc(pace, 1)
                    here = same[:, bass.ds(k * CHUNK, CHUNK)]
                    for h in range(4):
                        last = nc.vector.tensor_tensor_scan(ad[s][:, :, h], here, ad[s][:, :, h], ad_last[:, h:h + 1], ALU.mult, ALU.add)
                    ch.done(last)
                    ch.done(nc.vector.tensor_copy(ad_last[:, :], ad[s][:, CHUNK - 1, :]))
                    ch.done(nc.vector.tensor_scalar(same_neg[:, :], here, -1.0, -LOW, ALU.add, ALU.mult))
                    v.wait_ge(gathered[s], (k2 + 1) * 16 * CHUNK)
                    ch.done(nc.vector.tensor_tensor(score[:, :, :], E[s][:, :, 20:24], ad[s][:, :, :], ALU.add))
                    ch.done(nc.vector.scalar_tensor_tensor(score[:, :, :], score[:, :, :], 0.2, score[:, :, :], ALU.mult, ALU.max))
                    v.sem_inc(gat_free, 1)
                    nc.vector.tensor_copy(idx[s][:, :], src[:, bass.ds(k * CHUNK + 2 * CHUNK, CHUNK)]).then_inc(idx_ready, 1)
                    segment_run(E[s], top, score[:, :, :], same_neg[:, :], X, lambda c: sum_last[:, c:c + 1],
                                x_ready, exp_ready, k + 1)
                    ch.done(nc.vector.tensor_copy(top[:, 0:1, :], top[:, CHUNK:CHUNK + 1, :]))
                    ch.done(nc.vector.tensor_copy(sum_last[:, :], E[s][:, CHUNK - 1, 0:20]))
                    v.sem_inc(rows_ready, 1)
                    k_used = ch.n
            assert k_used == K, k_used
            ch.start(base + CHUNKS * K)
            nc.vector.tensor_copy(tail[:, 0:20], sum_last[:, :])
            ch.done(nc.vector.tensor_copy(tail[:, 20:24], top[:, 0, :]))
            v.sem_inc(tail_ready, 1)
            v.wait_ge(place_ready, 1)
            ch.done(nc.vector.tensor_copy(place[:, 0:1], dst[:, 0:1]))
            is_first = X[:, :, :, :].rearrange("p a f h -> p (a f h)")
            ch.done(nc.vector.tensor_scalar(is_first, dst[:, :], place[:, 0:1], None, ALU.is_equal))
            ch.done(nc.vector.tensor_reduce(place[:, 1:2], is_first, AX, ALU.add))
            ch.done(nc.vector.tensor_copy(place[:, 2:3], place_i[:, 0:1]))
            ch.done(nc.vector.tensor_scalar(place[:, 1:2], place[:, 1:2], place[:, 2:3], -1.0 - SKIP, ALU.add, ALU.add))
            ch.done(nc.vector.tensor_scalar(place[:, 1:2], place[:, 1:2], same[:, 0:1], float(SKIP), ALU.mult, ALU.add))
            ch.done(nc.vector.tensor_copy(place_i[:, 1:2], place[:, 1:2]))
            v.sem_inc(place_ready, 2)
            ch.done(nc.vector.memset(chain_top[:, 0:1, :], LOW))
            ch.done(nc.vector.memset(link[:, 0, 0:1], 0.0))
            ch.done(nc.vector.tensor_tensor(link[:, 0, 1:128], ends16[:, 0, 1:128], ends16[:, 1, 0:127], ALU.is_equal))
            ch.done(nc.vector.tensor_tensor(link[:, 1, :], ends16[:, 0, :], ends16[:, 1, :], ALU.is_equal))
            ch.done(nc.vector.tensor_tensor(link[:, 0, :], link[:, 0, :], link[:, 1, :], ALU.mult))
            ch.done(nc.vector.tensor_scalar(link[:, 2, :], link[:, 0, :], -1.0, -LOW, ALU.add, ALU.mult))
            v.wait_ge(chain_in, 16)
            segment_run(chain[:, :, :], chain_top, chain[:, :, 20:24], link[:, 2, :], chain_x, lambda c: 0.0,
                        chain_x_ready, chain_exp, 1)
            v.sem_inc(carry_ready, 1)
            for s in range(2):
                v.wait_ge(runs_out[s], CHUNKS * 8)
            ch.done(nc.vector.memset(t["edge_rows"][:, :], 0.0))
            ch.done(nc.vector.memset(node_run[:, :, 20:24], LOW))
            v.sem_inc(init_ready, 1)
            v.wait_ge(carry_in, 16)
            v.wait_ge(patch_in, 16)
            ch.done(nc.vector.tensor_tensor(px[:, 0, :], patch[:, 20:24], carry[:, 20:24], ALU.max))
            nc.vector.tensor_tensor(px[:, 1, :], patch[:, 20:24], px[:, 0, :], ALU.subtract)
            ch.done(nc.vector.tensor_tensor(px[:, 2, :], carry[:, 20:24], px[:, 0, :], ALU.subtract))
            v.sem_inc(px_ready, 1)
            v.wait_ge(px_exp, 1)
            for k, tile in ((1, patch), (2, carry)):
                sums = tile[:, 0:20].rearrange("p (h v) -> p h v", v=5)
                ch.done(nc.vector.tensor_tensor(sums, sums, bc(px[:, k, :], 2, 5), ALU.mult))
            ch.done(nc.vector.tensor_tensor(patch[:, 0:20], patch[:, 0:20], carry[:, 0:20], ALU.add))
            ch.done(nc.vector.tensor_copy(patch[:, 20:24], px[:, 0, :]))
            v.sem_inc(patch_ready, 1)


def combine(nc, t, dram):
    node_run = t["edge_rows"][:, :].rearrange("p (c v) -> p c v", v=ROW)
    C = 64
    out_rows = dram["out"].rearrange("b (c p) d -> b p c d", p=128)
    with ExitStack() as ctx:
        sem = lambda n: ctx.enter_context(nc.semaphore(n))
        sb = lambda n, s, d=F32: ctx.enter_context(nc.sbuf_tensor(n, s, d))
        nd = [sb(f"nd{i}", [128, C, ROW]) for i in range(2)]
        X = sb("rx", [128, 2, C, 4])
        own, high = sb("own", [128, C, 4]), sb("high", [128, C, 4])
        agg, agg2 = sb("agg", [128, C, 16]), sb("agg2", [128, C, 16])
        den = sb("den", [128, C, 4])
        m1, m2 = sb("m1", [128, C]), sb("m2", [128, C])
        sc, sel = sb("r_score", [128, C, 4]), sb("r_sel", [128, C, 4])
        beats = sb("beats", [128, C, 4, 3])
        gate = sb("gate", [128, NODE_TILES, 4])
        const = sb("r_const", [128, 3, 16])
        ex = [sb(f"ex{i}", [128, 4, 16, 64]) for i in range(2)]
        hb = [sb(f"hb{i}", [128, 16, 64]) for i in range(2)]
        part = [sb(f"part{i}", [128, 2, 16, 64]) for i in range(2)]
        const_in, dve, x_ready, exp_ready, std_ready, var_ready, nd_free, ex_free, pool_done, prod_ready, sum_ready = (
            sem(n) for n in ("const_in", "r_dve", "rx_ready", "rexp_ready", "rstd_ready", "rvar_ready", "nd_free",
                             "ex_free", "pool_done", "prod_ready", "sum_ready"))
        nd_in = [sem("nd_in0"), sem("nd_in1")]
        ex_in = [sem("ex_in0"), sem("ex_in1")]
        out_done = [sem("out_done0"), sem("out_done1")]
        block = ctx.enter_context(nc.Block())
        G = NODE_TILES // C

        @block.sync
        def _(sp):
            for k, name in enumerate(("b_gat", "ln_gamma", "ln_beta")):
                sp.dma_start(const[:, k, :], dram[name].rearrange("(a n) -> a n", a=1).to_broadcast([128, 16])).then_inc(const_in, 16)
            with sp.Fori(0, G // 2) as k2:
                for s in range(2):
                    k = k2 * 2 + s
                    sp.wait_ge(nd_free, k + 1)
                    sp.dma_start(nd[s][:, :, :].rearrange("p (b c) v -> p b (c v)", b=4),
                                 dram["node_own"][bass.ds(k * 4, 4)].rearrange("b p c v -> p b (c v)")).then_inc(nd_in[s], 16)
            with sp.Fori(0, 16) as n2:
                for s in range(2):
                    n = n2 * 2 + s
                    sp.wait_ge(ex_free, n + 1)
                    sp.dma_start(ex[s][:, :, :, :].rearrange("p e c d -> p (e c d)"),
                                 dram["experts"][bass.ds(n, 1)].rearrange("a p v -> (a p) v")).then_inc(ex_in[s], 16)
                    sp.wait_ge(out_done[s], n2 * 16)
                    sp.dma_start(hb[s][:, :, :].rearrange("p c d -> p (c d)"),
                                 dram["h2"][bass.ds(n, 1)].rearrange("a p c d -> (a p) (c d)")).then_inc(ex_in[s], 16)

        @block.scalar
        def _(act):
            with act.Fori(0, G) as k:
                act.wait_ge(x_ready, 2 * k + 1)
                act.activation(X[:, :, :, :], X[:, :, :, :], ACT.Exp).then_inc(exp_ready, 1)
                act.wait_ge(var_ready, k + 1)
                act.activation(m1[:, :], m2[:, :], ACT.Sqrt).then_inc(std_ready, 1)
                act.wait_ge(x_ready, 2 * k + 2)
                act.activation(X[:, 0, :, :], X[:, 0, :, :], ACT.Exp).then_inc(exp_ready, 1)
            with act.Fori(0, 16) as n2:
                for s in range(2):
                    act.wait_ge(sum_ready, n2 * 2 + s + 1)
                    act.dma_start(out_rows[bass.ds(n2 * 2 + s, 1)].rearrange("a p c d -> (a p) c d"), hb[s][:, :, :]).then_inc(out_done[s], 16)
            for s in range(2):
                act.wait_ge(out_done[s], 256)

        @block.gpsimd
        def _(pool):
            with pool.Fori(0, 16) as n2:
                for s in range(2):
                    n = n2 * 2 + s
                    pool.wait_ge(prod_ready, 2 * n + 1)
                    nc.gpsimd.tensor_tensor(ex[s][:, 0, :, :], ex[s][:, 0, :, :], ex[s][:, 1, :, :], ALU.add).then_inc(pool_done, 1)

        @block.vector
        def _(v):
            ch = Chain(v, dve)
            v.sem_inc(nd_free, 2)
            v.sem_inc(ex_free, 2)
            v.wait_ge(const_in, 48)
            wide = lambda k: bc(const[:, k, :], 1, C)
            flat16 = lambda a: a[:, :, :]
            K = 31
            with v.Fori(0, G // 2) as k2:
                for s in range(2):
                    k = k2 * 2 + s
                    ch.start(k * K)
                    v.wait_ge(nd_in[s], (k2 + 1) * 16)
                    here = node_run[:, bass.ds(k * C, C), :]
                    ch.done(nc.vector.tensor_tensor(own[:, :, :], nd[s][:, :, 20:24], nd[s][:, :, 24:28], ALU.add))
                    ch.done(nc.vector.scalar_tensor_tensor(own[:, :, :], own[:, :, :], 0.2, own[:, :, :], ALU.mult, ALU.max))
                    ch.done(nc.vector.tensor_tensor(high[:, :, :], own[:, :, :], here[:, :, 20:24], ALU.max))
                    nc.vector.tensor_tensor(X[:, 0, :, :], own[:, :, :], high[:, :, :], ALU.subtract)
                    ch.done(nc.vector.tensor_tensor(X[:, 1, :, :], here[:, :, 20:24], high[:, :, :], ALU.subtract))
                    v.sem_inc(x_ready, 1)
                    v.wait_ge(exp_ready, 2 * k + 1)
                    a = nd[s][:, :, 0:20].rearrange("p c (h v) -> p c h v", v=5)
                    b = here[:, :, 0:20].rearrange("p c (h v) -> p c h v", v=5)
                    nc.vector.tensor_tensor(a, a, bc(X[:, 0, :, :], 3, 5), ALU.mult)
                    ch.done(nc.vector.tensor_tensor(b, b, bc(X[:, 1, :, :], 3, 5), ALU.mult))
                    ch.done(nc.vector.tensor_tensor(a, a, b, ALU.add))
                    ch.done(nc.vector.tensor_scalar(den[:, :, :], a[:, :, :, 0], 1e-16, None, ALU.add))
                    ch.done(nc.vector.reciprocal(den[:, :, :], den[:, :, :]))
                    g4 = agg[:, :, :].rearrange("p c (h v) -> p c h v", v=4)
                    ch.done(nc.vector.tensor_tensor(g4, a[:, :, :, 1:5], bc(den[:, :, :], 3, 4), ALU.mult))
                    v.sem_inc(nd_free, 1)
                    ch.done(nc.vector.tensor_tensor(agg[:, :, :], agg[:, :, :], wide(0), ALU.add))
                    ch.done(nc.vector.tensor_reduce(m1[:, :], agg[:, :, :], AX, ALU.add))
                    ch.done(nc.vector.tensor_scalar(m1[:, :], m1[:, :], 1.0 / 16, None, ALU.mult))
                    ch.done(nc.vector.tensor_tensor(agg[:, :, :], agg[:, :, :], bc(m1[:, :], 2, 16), ALU.subtract))
                    ch.done(nc.vector.tensor_tensor(agg2[:, :, :], agg[:, :, :], agg[:, :, :], ALU.mult))
                    ch.done(nc.vector.tensor_reduce(m2[:, :], agg2[:, :, :], AX, ALU.add))
                    ch.done(nc.vector.tensor_scalar(m2[:, :], m2[:, :], 1.0 / 16, 1e-5, ALU.mult, ALU.add))
                    v.sem_inc(var_ready, 1)
                    v.wait_ge(std_ready, k + 1)
                    ch.done(nc.vector.reciprocal(m1[:, :], m1[:, :]))
                    ch.done(nc.vector.tensor_tensor(agg[:, :, :], agg[:, :, :], bc(m1[:, :], 2, 16), ALU.mult))
                    ch.done(nc.vector.tensor_tensor(agg[:, :, :], agg[:, :, :], wide(1), ALU.mult))
                    ch.done(nc.vector.tensor_tensor(agg[:, :, :], agg[:, :, :], wide(2), ALU.add))
                    ch.done(nc.vector.tensor_reduce(sc[:, :, :], agg[:, :, :].rearrange("p c (h v) -> p c v h", v=4), AX, ALU.add))
                    ch.done(nc.vector.tensor_scalar(sc[:, :, :], sc[:, :, :], 0.25, None, ALU.mult))
                    for e in range(4):
                        for q, o in enumerate(x for x in range(4) if x != e):
                            last = nc.vector.tensor_tensor(beats[:, :, e, q], sc[:, :, o], sc[:, :, e], ALU.is_ge if o < e else ALU.is_gt)
                    ch.done(last)
                    ch.done(nc.vector.tensor_reduce(sel[:, :, :], beats[:, :, :, :], AX, ALU.add))
                    ch.done(nc.vector.tensor_scalar(sel[:, :, :], sel[:, :, :], 1.5, None, ALU.is_lt))
                    ch.done(nc.vector.tensor_reduce(m1[:, :], sc[:, :, :], AX, ALU.max))
                    ch.done(nc.vector.tensor_tensor(X[:, 0, :, :], sc[:, :, :], bc(m1[:, :], 2, 4), ALU.subtract))
                    v.sem_inc(x_ready, 1)
                    v.wait_ge(exp_ready, 2 * k + 2)
                    ch.done(nc.vector.tensor_tensor(sel[:, :, :], sel[:, :, :], X[:, 0, :, :], ALU.mult))
                    ch.done(nc.vector.tensor_reduce(m1[:, :], sel[:, :, :], AX, ALU.add))
                    ch.done(nc.vector.reciprocal(m1[:, :], m1[:, :]))
                    ch.done(nc.vector.tensor_tensor(gate[:, bass.ds(k * C, C), :], sel[:, :, :], bc(m1[:, :], 2, 4), ALU.mult))
                    k_used = ch.n
            assert k_used == K, k_used
            base = G * K
            KB = 3
            with v.Fori(0, 16) as n2:
                for s in range(2):
                    n = n2 * 2 + s
                    ch.start(base + n * KB)
                    v.wait_ge(ex_in[s], (n2 + 1) * 32)
                    gates = gate[:, bass.ds(n * 16, 16), :]
                    for e in range(4):
                        last = nc.vector.tensor_tensor(ex[s][:, e, :, :], ex[s][:, e, :, :], bc(gates[:, :, e], 2, 64), ALU.mult)
                        if e % 2:
                            last.then_inc(prod_ready, 1)
                    v.wait_ge(prod_ready, 2 * n + 2)
                    ch.done(nc.vector.tensor_tensor(ex[s][:, 2, :, :], ex[s][:, 2, :, :], ex[s][:, 3, :, :], ALU.add))
                    ch.done(nc.vector.tensor_tensor(hb[s][:, :, :], hb[s][:, :, :], ex[s][:, 2, :, :], ALU.add))
                    v.wait_ge(pool_done, n + 1)
                    ch.done(nc.vector.tensor_tensor(hb[s][:, :, :], hb[s][:, :, :], ex[s][:, 0, :, :], ALU.add))
                    v.sem_inc(sum_ready, 1)
                    v.sem_inc(ex_free, 1)


def tensors(nc, ctx):
    sb = lambda n, s, d=F32: ctx.enter_context(nc.sbuf_tensor(n, s, d))
    return dict(ident=sb("ident", [128, 128]), ones=sb("ones", [128, 128]), before=sb("before", [128, 128]),
                halves=sb("halves", [128, 128]), stat_w=sb("stat_w", [128, 4]), reset=sb("reset", [128, 8, 32]),
                rowbase=sb("rowbase", [128, 32]), bias_s=sb("bias_s", [128, 1]), bound=sb("bound", [128, 1]),
                w_cat=sb("w_cat", [64, ROW]), w12=sb("w12", [128, 64]), bias4=sb("bias4", [1, 256]),
                m0=sb("m0", [128, 1]), unit=sb("unit", [128, ROW]),
                first_edge=sb("first_edge", [128, NODE_TILES], I32), last_edge=sb("last_edge", [128, NODE_TILES], I32),
                busy=sb("busy", [1, NODE_TILES // SKIP_GROUP], I32))


def program(nc, dram):
    with ExitStack() as ctx:
        t = tensors(nc, ctx)
        make_constants(nc, t, dram)
        select_tokens(nc, t, dram)
        sort_edges(nc, t, dram)
        count_edges(nc, t, dram)
        attend(nc, t, dram)
        with nc.sbuf_tensor("edge_rows", [128, 2 * CHUNK * ROW], F32) as rows:
            t["edge_rows"] = rows
            pass_messages(nc, t, dram)
            combine(nc, t, dram)


SCRATCH = {"kept": ((M_NODES, 64), F32), "lag_rows": ((128, 64, LAG_W), F32), "h2": ((32, 128, 16, 64), F32),
           "node": ((M_NODES, ROW), F32), "node_own": ((32, 128, 16, ROW), F32), "x3t": ((64, M_NODES), F32),
           "sort_scratch": ((2, 128, COLS), U16), "sorted_dst": ((128, COLS), U16), "sorted_src": ((128, COLS), U16),
           "edge_ad": ((N_EDGES, 4), F32), "runs": ((N_EDGES, ROW), F32), "experts": ((32, 128, 4096), F32),
           "tails": ((128, ROW), F32), "carries": ((128, ROW), F32), "nothing": ((2, NODE_TILES // SKIP_GROUP, 1), I32)}
INPUTS = {"x": "x", "norm_w": "L0_tok_norm_w", "norm_b": "L0_tok_norm_b", "fc_w": "L0_tok_fc_w", "fc_b": "L0_tok_fc_b",
          "A_W1": "L0_attn_W1", "A_W2": "L0_attn_W2", "A_bias": "L0_attn_bias", "mem": "L0_attn_memory_weights",
          "W_gat": "L0_ffn_W_gat", "att_src": "L0_ffn_att_src", "att_dst": "L0_ffn_att_dst", "b_gat": "L0_ffn_b_gat",
          "ln_gamma": "L0_ffn_ln_gamma", "ln_beta": "L0_ffn_ln_beta", "F_W1": "L0_ffn_W1", "F_b1": "L0_ffn_b1",
          "F_W2": "L0_ffn_W2", "F_b2": "L0_ffn_b2", "edges": "L0_ffn_edge_index"}


def kernel(**inputs):
    import numpy as _np
    import concourse.bacc as _bacc
    from concourse import mybir as _mybir
    from concourse.bass_utils import run_bass_kernel_spmd as _run

    nc = _bacc.Bacc("TRN2", target_bir_lowering=False, num_devices=1)
    arrays, dram = {}, {}
    for name, given in INPUTS.items():
        a = _np.ascontiguousarray(inputs[given])
        arrays[f"in_{name}"] = a
        dram[name] = nc.dram_tensor(f"in_{name}", a.shape, _mybir.dt.from_np(a.dtype), kind="ExternalInput").ap()
    for name, (shape, dt) in SCRATCH.items():
        dram[name] = nc.dram_tensor(name, shape, dt, kind="Internal").ap()
    dram["out"] = nc.dram_tensor("out_0", (32, 2048, 64), F32, kind="ExternalOutput").ap()
    program(nc, dram)
    r = _run(nc, [arrays], core_ids=[0])
    return r.results[0]["out_0"]
```

```python
import numpy as np
import concourse.bass as bass
from concourse import mybir
from contextlib import ExitStack

F32 = mybir.dt.float32
I32 = mybir.dt.int32
ALU = mybir.AluOpType
ACT = mybir.ActivationFunctionType
AX = mybir.AxisListType.X
U16 = mybir.dt.uint16
BF16 = mybir.dt.bfloat16
LAG_W = 256
M_NODES, N_EDGES = 65536, 262144
COLS = N_EDGES // 128
NODE_TILES = M_NODES // 128
SKIP_GROUP = 8
SKIP = 1 << 20
LOW = -1e30


class Chain:

    def __init__(self, eng, sem):
        self.eng, self.sem, self.base, self.n = eng, sem, 0, 0

    def done(self, ins, apart=None):
        ins.then_inc(self.sem, 1)
        self.n += 1
        self.eng.wait_ge(self.sem, self.base + self.n)
        if apart is not None:
            self.eng.sem_inc(apart, 1)

    def start(self, base):
        self.base, self.n = base, 0


def bc(ap, dim, count):
    return ap.unsqueeze(dim).to_broadcast([*ap.shape[:dim], count, *ap.shape[dim:]])


def make_constants(nc, t, dram):
    with ExitStack() as ctx:
        sem = lambda n: ctx.enter_context(nc.semaphore(n))
        sb = lambda n, s, d=F32: ctx.enter_context(nc.sbuf_tensor(n, s, d))
        ps = ctx.enter_context(nc.psum_tensor("prep_psum", [128, 512], F32))
        small_in, built, mean_ready, used, dve = (sem(n) for n in
            ("small_in", "built", "mean_ready", "centred", "prep_dve"))
        rows_out = sem("rows_out")
        raw = sb("raw", [128, 8])
        cols = sb("cols", [128, 4])
        mem_t = sb("mem_t", [64, 41])
        rows = sb("rows", [64, LAG_W])
        wg = sb("wg", [64, 16])
        att = sb("att", [64, 2, 16])
        prod = sb("prod", [64, 2, 16])
        block = ctx.enter_context(nc.Block())

        @block.sync
        def _(sp):
            column = lambda v: v.rearrange("(d one) -> d one", one=1)
            for half in range(2):
                h = slice(64 * half, 64 * half + 64)
                sp.dma_start(raw[h, 0:1], column(dram["norm_w"])).then_inc(small_in, 16)
                sp.dma_start(raw[h, 1:2], column(dram["norm_b"])).then_inc(small_in, 16)
                sp.dma_start(raw[h, 2:3], dram["fc_w"].rearrange("one d -> d one"), allow_slow_non_contiguous=True).then_inc(small_in, 16)
            sp.dma_start(raw[:, 3:4], dram["fc_b"].rearrange("(a b) -> a b", a=1).to_broadcast([128, 1])).then_inc(small_in, 16)
            sp.dma_start(mem_t[:, :], dram["mem"].rearrange("l d -> d l"), allow_slow_non_contiguous=True).then_inc(small_in, 16)
            sp.dma_start(wg[:, :], dram["W_gat"]).then_inc(small_in, 16)
            for k, name in enumerate(("att_src", "att_dst")):
                sp.dma_start(att[:, k, :], dram[name].rearrange("h e -> (h e)").rearrange("(a n) -> a n", a=1)
                             .to_broadcast([64, 16])).then_inc(small_in, 16)
            sp.dma_start(t["w12"][0:64, :], dram["A_W1"]).then_inc(small_in, 16)
            sp.dma_start(t["w12"][64:128, :], dram["A_W2"]).then_inc(small_in, 16)
            sp.dma_start(t["bias4"][:, :].rearrange("a (r n) -> a r n", r=4),
                         bc(dram["A_bias"].rearrange("(a n) -> a n", a=1), 1, 4)).then_inc(small_in, 16)
            sp.dma_start(t["m0"][64:128, :], dram["mem"][0, :].rearrange("(d one) -> d one", one=1)).then_inc(small_in, 16)
            sp.wait_ge(dve, 5)
            sp.dma_start(dram["lag_rows"].rearrange("k d x -> d k x"), bc(rows[:, :], 1, 128)).then_inc(rows_out, 16)
            sp.wait_ge(rows_out, 16)

        @block.gpsimd
        def _(pool):
            nc.gpsimd.memset(t["ident"][:, :], 0.0).then_inc(built, 1)
            nc.gpsimd.memset(t["ones"][:, :], 1.0).then_inc(built, 1)
            nc.gpsimd.memset(t["before"][:, :], 1.0).then_inc(built, 1)
            nc.gpsimd.memset(t["halves"][:, :], 0.0).then_inc(built, 1)
            nc.gpsimd.memset(t["stat_w"][:, :], 0.0).then_inc(built, 1)
            pool.wait_ge(built, 5)
            nc.gpsimd.affine_select(out=t["ident"][:, :], in_=t["ident"][:, :], compare_op=ALU.not_equal,
                                    fill=1.0, base=0, pattern=[[-1, 128]], channel_multiplier=1).then_inc(built, 1)
            nc.gpsimd.affine_select(out=t["before"][:, :], in_=t["before"][:, :], compare_op=ALU.is_gt,
                                    fill=0.0, base=0, pattern=[[1, 128]], channel_multiplier=-1).then_inc(built, 1)
            for half in range(2):
                h = slice(64 * half, 64 * half + 64)
                pool.wait_ge(built, 7 + 2 * half)
                nc.gpsimd.memset(t["halves"][h, h], 1.0 / 64).then_inc(built, 1)
                pool.wait_ge(built, 8 + 2 * half)
                nc.gpsimd.memset(t["stat_w"][h, 2 + half:3 + half], 1.0 / 64).then_inc(built, 1)
            pool.wait_ge(built, 11)
            nc.gpsimd.memset(t["reset"][:, :, :], 1.0).then_inc(built, 1)
            pool.wait_ge(built, 12)
            nc.gpsimd.memset(t["reset"][:, :, 0:1], 0.0).then_inc(built, 1)
            nc.gpsimd.iota(t["rowbase"][:, :], pattern=[[2048, 32]], base=0, channel_multiplier=0,
                           allow_small_or_imprecise_dtypes=True).then_inc(built, 1)

        @block.vector
        def _(v):
            ch = Chain(v, dve)
            v.wait_ge(small_in, 16 * 15)
            ch.done(nc.vector.tensor_tensor(cols[:, 0:1], raw[:, 0:1], raw[:, 2:3], ALU.mult))
            ch.done(nc.vector.tensor_tensor(cols[:, 1:2], raw[:, 1:2], raw[:, 2:3], ALU.mult))
            ch.done(nc.vector.memset(rows[:, :], 0.0))
            ch.done(nc.vector.tensor_copy(raw[0:64, 4:5], mem_t[:, 0:1]))
            ch.done(nc.vector.tensor_scalar(rows[:, 128:168], mem_t[:, 1:41], mem_t[:, 0:1], None, ALU.subtract))
            v.wait_ge(mean_ready, 1)
            ch.done(nc.vector.tensor_copy(cols[:, 2:4], ps[:, 0:2]))
            ch.done(nc.vector.tensor_tensor(cols[:, 0:1], cols[:, 0:1], cols[:, 2:3], ALU.subtract))
            ch.done(nc.vector.tensor_tensor(cols[:, 1:2], cols[:, 0:1], cols[:, 0:1], ALU.mult)
                    )
            v.wait_ge(built, 14)
            ch.done(nc.vector.tensor_copy(t["stat_w"][0:64, 0:1], cols[0:64, 0:1]))
            ch.done(nc.vector.tensor_copy(t["stat_w"][64:128, 1:2], cols[64:128, 0:1]))
            ch.done(nc.vector.tensor_scalar(t["bias_s"][:, :], cols[:, 3:4], 64.0, raw[:, 3:4], ALU.mult, ALU.add))
            nc.vector.tensor_copy(cols[:, 2:3], cols[:, 1:2]).then_inc(used, 1)
            v.wait_ge(mean_ready, 2)
            ch.done(nc.vector.tensor_copy(t["bound"][:, :], ps[:, 2:3]))
            ch.done(nc.vector.memset(t["unit"][:, :], 0.0))
            ch.done(nc.vector.memset(t["unit"][:, 0:20].rearrange("p (h v) -> p h v", v=5)[:, :, 0:1], 1.0))
            ch.done(nc.vector.memset(t["w_cat"][:, :], 0.0))
            ch.done(nc.vector.tensor_copy(
                t["w_cat"][:, 0:20].rearrange("d (h v) -> d h v", v=5)[:, :, 1:5],
                wg[:, :].rearrange("d (h v) -> d h v", v=4)))
            ch.done(nc.vector.tensor_tensor(prod[:, :, :], att[:, :, :], bc(wg[:, :], 1, 2), ALU.mult))
            ch.done(nc.vector.tensor_reduce(t["w_cat"][:, 20:28].rearrange("d (k h) -> d k h", k=2),
                                            prod[:, :, :].rearrange("d k (h v) -> d k h v", v=4), AX, ALU.add))

        @block.tensor
        def _(pe):
            pe.wait_ge(built, 14)
            pe.wait_ge(dve, 2)
            nc.tensor.matmul(ps[:, 0:2], t["halves"][:, :], cols[:, 0:2], start=True, stop=True).then_inc(mean_ready, 1)
            pe.wait_ge(used, 1)
            nc.tensor.matmul(ps[:, 2:3], t["halves"][:, :], cols[:, 2:3], start=True, stop=True).then_inc(mean_ready, 1)

        @block.scalar
        def _(act):
            act.wait_ge(dve, 12)
            act.activation(t["bound"][:, :], t["bound"][:, :], ACT.Sqrt, scale=64.0 * 64.0 * 1.01).then_inc(used, 1)
            act.wait_ge(used, 2)


def phase_stages():
    step = 0
    for k in range(1, 19):
        for j in range(k - 1, -1, -1):
            yield step, k, j
            step += 1


def crossings():
    return [step for step, k, j in phase_stages() if k > 11 and j in (k - 1, 10)]


def select_and_sort(nc, t, dram):
    x2 = dram["x"].rearrange("(q b) d h w -> q (b d) (h w)", b=2)
    with ExitStack() as ctx:
        sem = lambda n: ctx.enter_context(nc.semaphore(n))
        sb = lambda n, s, d=F32: ctx.enter_context(nc.sbuf_tensor(n, s, d))
        pt = lambda n, s: ctx.enter_context(nc.psum_tensor(n, s, F32))
        ident, ones, before = t["ident"], t["ones"], t["before"]
        xt = [sb(f"image{i}", [128, 4096]) for i in range(2)]
        T = [sb(f"tokens{i}", [128, 8, 32, 64]) for i in range(2)]
        idx = [sb(f"place{i}", [128, 256], I32) for i in range(2)]
        stats = sb("stats", [128, 3, 8, 32])
        dot, mu, ss = (stats[:, k, :, :] for k in range(3))
        big = lambda n: sb(n, [128, 8, 32])
        sc, a1, a2, tie, sel, run = (big(n) for n in ("score", "tmp1", "tmp2", "tie", "sel", "run"))
        small = lambda n: sb(n, [128, 8])
        lo, hi, cnt, need, tot, side = (small(n) for n in ("lo", "hi", "cnt", "need", "tot", "side"))
        mid = [small(f"mid{i}") for i in range(2)]
        reach, step_now = sb("reach", [128, 1]), sb("step_now", [128, 1])
        side0 = small("side0")
        geq = sb("geq", [128, 8], I32)
        lss = sb("lss", [128, 8], I32)
        tp = [pt(f"tp{i}", [128, 4, 2, 64]) for i in range(4)]
        stp = [pt(f"stp{i}", [128, 32, 6]) for i in range(2)]
        cp = pt("cp", [128, 8])
        loaded = [sem("image_in0"), sem("image_in1")]
        image_free, tp_ready, tp_free, sums_ready, squared, st_ready, st_free = (sem(n) for n in
            ("image_free", "tp_ready", "tp_free", "sums_ready", "squared", "st_ready", "st_free"))
        stats_ready, stats_used, var_ready, std_ready = (sem(n) for n in ("stats_ready", "stats_used", "var_ready", "std_ready"))
        cnt_ready, cnt_out, dve, idx_ready = (sem(n) for n in ("cnt_ready", "cnt_out", "sel_dve", "idx_ready"))
        sent = [sem("kept_out0"), sem("kept_out1")]
        tokens_free, pace, pace_pool, reach_dve = sem("tokens_free"), sem("pace"), sem("pace_pool"), sem("reach_dve")
        key = [sb(f"key{i}", [128, COLS], U16) for i in range(2)]
        src = sb("src", [128, COLS], U16)
        raw = sb("raw_edges", [128, COLS], I32)
        swapped, delta = sb("swapped", [128, COLS // 2], U16), sb("delta", [128, COLS // 2], U16)
        pid, bit = sb("pid", [128, 8], I32), sb("bit", [128, 8])
        sign, off = sb("sign", [128, 9]), sb("off", [128, 9])
        edges_in, sort_dve, raw_used, pid_ready = (sem(n) for n in ("edges_in", "sort_dve", "raw_used", "pid_ready"))
        key_turned, src_turned, key_left, src_left, key_back, src_back = (sem(n) for n in
            ("key_turned", "src_turned", "key_left", "src_left", "key_back", "src_back"))
        cross = crossings()
        scratch = dram["sort_scratch"]
        ITER = 32
        GROUPS, PAIRS = 4, 4
        SUMS = ITER + 3
        TURN_TO = (41, 80, 109)
        block = ctx.enter_context(nc.Block())

        def groups(eng):
            with eng.Fori(0, GROUPS // 2) as g2:
                for gb in range(2):
                    yield g2, gb, g2 * 2 + gb

        @block.sync
        def _(sp):
            def images(first, last):
                with sp.Fori(first // 2, last // 2) as q:
                    for qb in range(2):
                        sp.wait_ge(image_free, q * 2 + qb + 1)
                        sp.dma_start(xt[qb][:, :], x2[bass.ds(q * 2 + qb, 1)].rearrange("a p n -> (a p) n")).then_inc(loaded[qb], 16)

            def turn(n):
                step = cross[n]
                for k, (tile, turned, left) in enumerate(((key[step % 2], key_turned, key_left), (src, src_turned, src_left))):
                    sp.wait_ge(turned, n + 1)
                    sp.dma_start(scratch[k], tile[:, :]).then_inc(left, 16)
                for k, (tile, left, back) in enumerate(((key[step % 2], key_left, key_back), (src, src_left, src_back))):
                    sp.wait_ge(left, 16 * (n + 1))
                    sp.dma_start(tile[:, :].rearrange("q (p l) -> q p l", l=16),
                                 scratch[k].rearrange("p (q l) -> q p l", l=16)).then_inc(back, 16)

            images(0, PAIRS)
            e = dram["edges"].rearrange("k (p f) -> k p f", p=128)
            sp.dma_start(raw[:, :], e[0]).then_inc(edges_in, 16)
            sp.wait_ge(raw_used, 1)
            sp.dma_start(raw[:, :], e[1]).then_inc(edges_in, 16)
            done = 0
            for g in range(1, GROUPS):
                images(g * PAIRS, (g + 1) * PAIRS)
                while cross[done] <= TURN_TO[g - 1]:
                    turn(done)
                    done += 1
            while done < len(cross):
                turn(done)
                done += 1
            sp.wait_ge(key_turned, len(cross) + 1)
            sp.dma_start(dram["sorted_dst"], key[171 % 2][:, :]).then_inc(key_left, 16)
            sp.wait_ge(src_turned, len(cross) + 1)
            sp.dma_start(dram["sorted_src"], raw[:, :]).then_inc(src_left, 16)
            sp.wait_ge(key_left, 16 * (len(cross) + 1))
            sp.wait_ge(src_left, 16 * (len(cross) + 1))

        @block.tensor
        def _(pe):
            pe.sem_inc(image_free, 2)
            for g2, gb, g in groups(pe):
                with pe.Fori(0, 2) as q2:
                    for qb in range(2):
                        pair = g * PAIRS + q2 * 2 + qb
                        pe.wait_ge(loaded[qb], (g * 2 + q2 + 1) * 16)
                        xv = xt[qb][:, :].rearrange("p (n c) -> p c n", c=32)
                        for c4 in range(8):
                            pe.wait_ge(tp_free, pair * 8 + c4 + 1)
                            for j in range(4):
                                last = nc.tensor.transpose(tp[c4 % 4][:, j, :, :].rearrange("p b d -> p (b d)"),
                                                           xv[:, c4 * 4 + j, :], ident[:, :])
                            last.then_inc(tp_ready, 1)
                        pe.wait_ge(st_free, pair + 1)
                        for c in range(32):
                            last = nc.tensor.matmul(stp[qb][:, c, 0:4], xv[:, c, :], t["stat_w"][:, :], start=True, stop=True)
                        last.then_inc(sums_ready, 1)
                        pe.wait_ge(squared, pair + 1)
                        for c in range(32):
                            last = nc.tensor.matmul(stp[qb][:, c, 4:6], xv[:, c, :], t["stat_w"][:, 2:4], start=True, stop=True)
                        last.then_inc(st_ready, 1)
                        pe.wait_ge(st_ready, pair + 1)
                        pe.sem_inc(image_free, 1)
                with pe.Fori(0, ITER) as i:
                    pe.wait_ge(cnt_ready, g * SUMS + i + 1)
                    nc.tensor.matmul(cp[:, :], ones[:, :], cnt[:, :], start=True, stop=True).then_inc(cnt_out, 1)
                pe.wait_ge(cnt_ready, g * SUMS + ITER + 1)
                nc.tensor.matmul(cp[:, :], ones[:, :], cnt[:, :], start=True, stop=True).then_inc(cnt_out, 1)
                for k in range(2):
                    pe.wait_ge(cnt_ready, g * SUMS + ITER + 2 + k)
                    nc.tensor.matmul(cp[:, :], before[:, :], tot[:, :], start=True, stop=True).then_inc(cnt_out, 1)

        @block.scalar
        def _(act):
            act.sem_inc(tp_free, 4)
            act.sem_inc(st_free, 2)
            for g2, gb, g in groups(act):
                act.wait_ge(tokens_free, g + 1)
                with act.Fori(0, 2) as q2:
                    for qb in range(2):
                        pair = g * PAIRS + q2 * 2 + qb
                        here = bass.ds(q2 * 4 + qb * 2, 2)
                        for c4 in range(8):
                            act.wait_ge(tp_ready, pair * 8 + c4 + 1)
                            act.activation(T[gb][:, here, c4 * 4:c4 * 4 + 4, :].rearrange("p b c d -> p c b d"),
                                           tp[c4 % 4][:, :, :, :], ACT.Copy).then_inc(tp_free, 1)
                        act.wait_ge(sums_ready, pair + 1)
                        act.activation(xt[qb][:, :], xt[qb][:, :], ACT.Square).then_inc(squared, 1)
                        act.wait_ge(st_ready, pair + 1)
                        act.wait_ge(stats_used, g + 1)
                        act.activation(stats[:, :, here, :].rearrange("p k b c -> p c k b"),
                                       stp[qb][:, :, :].rearrange("p c (k b) -> p c k b", b=2), ACT.Copy).then_inc(stats_ready, 1)
                        act.wait_ge(stats_ready, pair + 1)
                        act.sem_inc(st_free, 1)
                act.wait_ge(tp_free, (g + 1) * PAIRS * 8 + 4)
                act.wait_ge(var_ready, g + 1)
                act.activation(a2[:, :, :], a1[:, :, :], ACT.Sqrt).then_inc(std_ready, 1)

        @block.vector
        def _(v):
            v.sem_inc(stats_used, 1)
            ch = Chain(v, dve)
            K_ITER, K_REST = 5, 29
            per_group = K_ITER * ITER + K_REST
            scale = Chain(v, reach_dve)
            scale.done(nc.vector.memset(side0[:, :], 0.0))
            scale.done(nc.vector.scalar_tensor_tensor(reach[:, :], t["bias_s"][:, :], -1.0, t["bias_s"][:, :], ALU.mult, ALU.max))
            scale.done(nc.vector.tensor_scalar(reach[:, :], reach[:, :], t["bound"][:, :], 1e-30, ALU.add, ALU.max))
            bits = reach[:, :].bitcast(I32)
            scale.done(nc.vector.tensor_scalar(bits, bits, 23, None, ALU.logical_shift_right))
            scale.done(nc.vector.tensor_scalar(bits, bits, 23, None, ALU.logical_shift_left))
            scale.done(nc.vector.tensor_scalar(reach[:, :], reach[:, :], 2.0, None, ALU.mult))

            def select(g):
                gb = g % 2
                v.wait_ge(stats_ready, (g + 1) * PAIRS)
                ch.start(g * per_group)
                ch.done(nc.vector.tensor_tensor(a1[:, :, :], mu, mu, ALU.mult))
                ch.done(nc.vector.tensor_tensor(a1[:, :, :], ss, a1[:, :, :], ALU.subtract))
                ch.done(nc.vector.tensor_scalar(a1[:, :, :], a1[:, :, :], 0.0, 1e-5, ALU.max, ALU.add))
                v.sem_inc(var_ready, 1)
                v.wait_ge(std_ready, g + 1)
                ch.done(nc.vector.reciprocal(a2[:, :, :], a2[:, :, :]))
                ch.done(nc.vector.tensor_tensor(sc[:, :, :], dot, a2[:, :, :], ALU.mult))
                v.sem_inc(stats_used, 1)
                ch.done(nc.vector.tensor_scalar(sc[:, :, :], sc[:, :, :], t["bias_s"][:, :], None, ALU.add))
                nc.vector.tensor_scalar(lo[:, :], side0[:, :], reach[:, :], None, ALU.subtract)
                nc.vector.tensor_scalar(hi[:, :], side0[:, :], reach[:, :], None, ALU.add)
                nc.vector.tensor_copy(side[:, :], side0[:, :])
                nc.vector.tensor_copy(mid[0][:, :], side0[:, :])
                nc.vector.tensor_copy(mid[1][:, :], side0[:, :])
                ch.done(nc.vector.tensor_scalar(step_now[:, :], reach[:, :], 2.0, None, ALU.mult))
                first = g * per_group + 7
                v.sem_inc(pace, 1)

                def narrow(at):
                    nc.vector.tensor_scalar(geq[:, :], side[:, :], 0.0, None, ALU.is_gt)
                    nc.vector.tensor_scalar(step_now[:, :], step_now[:, :], 0.5, None, ALU.mult)
                    ch.done(nc.vector.tensor_scalar(lss[:, :], side[:, :], 0.0, None, ALU.is_lt), pace)
                    nc.vector.copy_predicated(lo[:, :], geq[:, :], at)
                    ch.done(nc.vector.copy_predicated(hi[:, :], lss[:, :], at), pace)

                with v.Fori(0, ITER // 2) as i2:
                    for h in range(2):
                        i = i2 * 2 + h
                        ch.start(first + i * K_ITER)
                        ch.done(nc.vector.tensor_tensor(a1[:, :, :], sc[:, :, :], bc(mid[h][:, :], 2, 32), ALU.is_ge))
                        nc.vector.tensor_reduce(cnt[:, :], a1[:, :, :], AX, ALU.add).then_inc(cnt_ready, 1)
                        narrow(mid[1 - h][:, :])
                        v.wait_ge(cnt_out, g * SUMS + i + 1)
                        ch.done(nc.vector.tensor_scalar(side[:, :], cp[:, :], 2047.5, 0.5, ALU.is_gt, ALU.subtract))
                        ch.done(nc.vector.scalar_tensor_tensor(mid[1 - h][:, :], side[:, :], step_now[:, :], mid[h][:, :], ALU.mult, ALU.add), pace)
                ch.start(first + ITER * K_ITER)
                narrow(mid[1][:, :])
                ch.done(nc.vector.tensor_tensor(sel[:, :, :], sc[:, :, :], bc(hi[:, :], 2, 32), ALU.is_ge))
                ch.done(nc.vector.tensor_tensor(tie[:, :, :], sc[:, :, :], bc(lo[:, :], 2, 32), ALU.is_ge))
                ch.done(nc.vector.tensor_tensor(tie[:, :, :], tie[:, :, :], sel[:, :, :], ALU.subtract))
                nc.vector.tensor_reduce(cnt[:, :], sel[:, :, :], AX, ALU.add).then_inc(cnt_ready, 1)
                v.wait_ge(cnt_out, g * SUMS + ITER + 1)
                ch.done(nc.vector.tensor_scalar(need[:, :], cp[:, :], -1.0, 2048.0, ALU.mult, ALU.add))

                def running(out, of, k):
                    flat = lambda a: a[:, :, :].rearrange("p b c -> p (b c)")
                    ch.done(nc.vector.tensor_tensor_scan(flat(out), flat(t["reset"]), flat(of), 0.0, ALU.mult, ALU.add))
                    nc.vector.tensor_copy(tot[:, :], out[:, :, 31]).then_inc(cnt_ready, 1)
                    v.wait_ge(cnt_out, g * SUMS + ITER + 2 + k)
                    ch.done(nc.vector.tensor_tensor(out[:, :, :], out[:, :, :], of[:, :, :], ALU.subtract))
                    ch.done(nc.vector.tensor_copy(cnt[:, :], cp[:, :]))
                    ch.done(nc.vector.tensor_tensor(out[:, :, :], out[:, :, :], bc(cnt[:, :], 2, 32), ALU.add))

                running(run, tie, 0)
                ch.done(nc.vector.tensor_tensor(a1[:, :, :], run[:, :, :], bc(need[:, :], 2, 32), ALU.is_lt))
                ch.done(nc.vector.tensor_tensor(a1[:, :, :], a1[:, :, :], tie[:, :, :], ALU.mult))
                ch.done(nc.vector.tensor_tensor(sel[:, :, :], sel[:, :, :], a1[:, :, :], ALU.add))
                running(run, sel, 1)
                ch.done(nc.vector.tensor_tensor(run[:, :, :], run[:, :, :],
                                                bc(t["rowbase"][:, g * 8:g * 8 + 8], 2, 32), ALU.add))
                ch.done(nc.vector.tensor_scalar(run[:, :, :], run[:, :, :], -131072.0, None, ALU.add))
                ch.done(nc.vector.tensor_tensor(run[:, :, :], run[:, :, :], sel[:, :, :], ALU.mult))
                ch.done(nc.vector.tensor_scalar(run[:, :, :], run[:, :, :], 131072.0, None, ALU.add))
                v.wait_ge(tokens_free, g + 1)
                ch.done(nc.vector.tensor_copy(idx[gb][:, :], run[:, :, :].rearrange("p b c -> p (b c)")))
                v.sem_inc(idx_ready, 1)
                assert ch.n + 7 == K_REST, ch.n + 7

            sort = Chain(v, sort_dve)

            def complement(part, column=None):
                if column is None:
                    sort.done(nc.vector.tensor_scalar(part, part, -1.0, 65535.0, ALU.mult, ALU.add))
                else:
                    sort.done(nc.vector.tensor_scalar(part, part, sign[:, column:column + 1], off[:, column:column + 1],
                                                      ALU.mult, ALU.add))

            def halves(tile, d):
                pairs = tile[:, :].rearrange("p (n t d) -> p n t d", t=2, d=d)
                return pairs[:, :, 0, :], pairs[:, :, 1, :]

            select(0)
            v.wait_ge(edges_in, 16)
            sort.done(nc.vector.tensor_copy(src[:, :], raw[:, :]))
            v.sem_inc(raw_used, 1)
            v.wait_ge(pid_ready, 1)
            for r in range(7):
                sort.done(nc.vector.tensor_scalar(pid[:, r:r + 1], pid[:, r:r + 1], r, 1,
                                                  ALU.logical_shift_right, ALU.bitwise_and))
            sort.done(nc.vector.tensor_copy(bit[:, 0:7], pid[:, 0:7]))
            sort.done(nc.vector.tensor_copy(sign[:, 0:1], bit[:, 0:1]))
            sort.done(nc.vector.tensor_scalar(sign[:, 1:2], bit[:, 0:1], -1.0, 1.0, ALU.mult, ALU.add))
            sort.done(nc.vector.tensor_tensor(sign[:, 2:8], bit[:, 0:6], bit[:, 1:7], ALU.not_equal))
            sort.done(nc.vector.tensor_copy(sign[:, 8:9], bit[:, 6:7]))
            sort.done(nc.vector.tensor_scalar(off[:, :], sign[:, :], 65535.0, None, ALU.mult))
            sort.done(nc.vector.tensor_scalar(sign[:, :], sign[:, :], -2.0, 1.0, ALU.mult, ALU.add))
            v.wait_ge(edges_in, 32)
            sort.done(nc.vector.tensor_copy(key[0][:, :], raw[:, :]))
            complement(key[0][:, :].rearrange("p (n f) -> p n f", f=4)[:, :, 2:4])
            for step, k, j in phase_stages():
                if step in TURN_TO:
                    select(TURN_TO.index(step) + 1)
                turned = step in cross
                turns_next = step + 1 in cross or step == 170
                if turned:
                    v.wait_ge(key_back, 16 * (cross.index(step) + 1))
                d = 1 << (j - 7 if j > 10 else j)
                a, b = halves(key[step % 2], d)
                low, high = halves(key[1 - step % 2], d)
                src_a, src_b = halves(src, d)
                m, x = (q[:, :].rearrange("p (n d) -> p n d", d=d) for q in (swapped, delta))
                nc.vector.tensor_tensor(m, a, b, ALU.is_gt)
                nc.vector.tensor_tensor(low, a, b, ALU.min)
                sort.done(nc.vector.tensor_tensor(high, a, b, ALU.max))
                if j == 0:
                    done = key[1 - step % 2]
                    if k < 10:
                        complement(done[:, :].rearrange("p (n f) -> p n f", f=4 << k)[:, :, 1 << k:3 << k])
                    elif k == 10:
                        complement(done[:, 0:1024], 0)
                        complement(done[:, 1024:2048], 1)
                    elif k < 18:
                        complement(done[:, :], k - 9)
                if turns_next:
                    v.sem_inc(key_turned, 1)
                if turned:
                    v.wait_ge(src_back, 16 * (cross.index(step) + 1))
                sort.done(nc.vector.tensor_tensor(x, src_a, src_b, ALU.bitwise_xor))
                sort.done(nc.vector.tensor_tensor(x, x, m, ALU.mult))
                nc.vector.tensor_tensor(src_a, src_a, x, ALU.bitwise_xor)
                sort.done(nc.vector.tensor_tensor(src_b, src_b, x, ALU.bitwise_xor))
                if step == 170:
                    sort.done(nc.vector.tensor_copy(raw[:, :], src[:, :]))
                if turns_next:
                    v.sem_inc(src_turned, 1)

        @block.gpsimd
        def _(pool):
            nc.gpsimd.iota(pid[:, :], pattern=[[0, 8]], base=0, channel_multiplier=1).then_inc(pid_ready, 1)
            pool.sem_inc(tokens_free, 2)
            for g2, gb, g in groups(pool):
                pool.wait_ge(idx_ready, g + 1)
                pool.sem_inc(pace_pool, 1)
                for b in range(8):
                    for c in range(32):
                        pool.indirect_dma_start(
                            out=dram["kept"], out_offset=bass.IndirectOffsetOnAxis(ap=idx[gb][:, b * 32 + c:b * 32 + c + 1], axis=0),
                            in_=T[gb][:, b, c, :], in_offset=None, bounds_check=65535, oob_is_err=False).then_inc(sent[gb], 16)
                pool.wait_ge(sent[gb], (g2 + 1) * 4096)
                pool.sem_inc(tokens_free, 1)


def attend(nc, t, dram):
    NB, NC, NG = 8, 16, 4
    PER = NB * NC
    kept = dram["kept"].rearrange("(b c p) d -> b p c d", p=128, c=NC)
    h2_rows = dram["h2"]
    node_own = dram["node_own"]
    node_rows = dram["node"].rearrange("(b c p) d -> b p c d", p=128, c=NC)
    with ExitStack() as ctx:
        sem = lambda n: ctx.enter_context(nc.semaphore(n))
        sb = lambda n, s, d=F32: ctx.enter_context(nc.sbuf_tensor(n, s, d))
        pt = lambda n, s: ctx.enter_context(nc.psum_tensor(n, s, F32))
        toep = sb("toep", [128, 64, 128])
        shared = sb("prev_and_xT", [128, 64 * 64])
        toep_prev = shared[:, :].rearrange("p (d m) -> p d m", m=64)
        xT = [shared[0:64, i * 2048:i * 2048 + 2048].rearrange("d (c p) -> d c p", p=128) for i in range(2)]
        H = [sb(f"H{i}", [128, NB, NC, 64]) for i in range(2)]
        Z = sb("Z", [128, NB, NC, 128])
        sq = sb("sq", [128, NC, 64])
        s1, s2, mean, rs, tmp = (sb(n, [128, NB, NC]) for n in ("s1", "s2", "mean", "rs", "lntmp"))
        zb = sb("zb", [128, NB])
        zt = [sb(f"zt{i}", [128, 4, 128]) for i in range(2)]
        y2 = sb("y2", [128, NC, 64])
        nrow = [sb(f"nrow{i}", [128, NC, 28]) for i in range(2)]
        t1, t2, t3, t4 = (sb(n, [128, NC]) for n in ("t1", "t2", "t3", "t4"))
        cps = [pt(f"cps{i}", [128, 4, NB, NC]) for i in range(2)]
        zp = [pt(f"zp{i}", [128, 4, 128]) for i in range(2)]
        op = [pt(f"op{i}", [128, 4, 64]) for i in range(2)]
        xp = pt("xp", [64, 4, 128])
        gp = pt("gp", [128, 512])
        tot_ps = gp[:, 448:448 + NB]
        node_ps = gp[:, 0:448].rearrange("p (c v) -> p c v", v=28)
        toep_in = sem("toep_in")
        h_in = [[sem(f"h_in{i}_{b}") for b in range(2)] for i in range(2)]
        h2_out = [sem("h2_out0"), sem("h2_out1")]
        x_out = [sem("x_out0"), sem("x_out1")]
        node_out = [sem("node_out0"), sem("node_out1")]
        (h_free, sq1, sq1_used, var1, std1, y_ready, tot_ready, zb_ready, conv_ready, conv_out, filt_ready,
         z_ready, zt_ready, o_ready, o_out, h2_ready, sq2, var2, std2, y2_ready, xp_ready, xp_out,
         gp_ready, gp_out, dve, pace, z_free) = (sem(n) for n in (
         "h_free", "sq1", "sq1_used", "var1", "std1", "y_ready", "tot_ready", "zb_ready", "conv_ready",
         "conv_out", "filt_ready", "z_ready", "zt_ready", "o_ready", "o_out", "h2_ready", "sq2", "var2", "std2",
         "y2_ready", "xp_ready", "xp_out", "gp_ready", "gp_out", "at_dve", "at_pace", "z_free"))
        block = ctx.enter_context(nc.Block())
        lag = dram["lag_rows"]

        @block.sync
        def _(sp):
            skew = 64 * LAG_W - 1
            sp.dma_start(toep[:, :, :], bass.AP(lag.tensor, 127, [[skew, 128], [LAG_W, 64], [1, 128]])).then_inc(toep_in, 16)
            sp.dma_start(toep_prev[64:128, :, :],
                         bass.AP(lag.tensor, 255 + 64 * skew, [[skew, 64], [LAG_W, 64], [1, 64]])).then_inc(toep_in, 16)
            with sp.Fori(0, 2) as g2:
                for gb in range(2):
                    g = g2 * 2 + gb
                    sp.wait_ge(h_free, g + 1)
                    for half in range(2):
                        b0 = half * 4
                        for b in range(4):
                            sp.dma_start(H[gb][:, b0 + b, :, :], kept[bass.ds(g * NB + b0 + b, 1)].rearrange("a p c d -> (a p) c d")
                                         ).then_inc(h_in[gb][half], 16)

        @block.tensor
        def _(pe):
            pe.wait_ge(toep_in, 32)
            pe.sem_inc(z_free, 1)
            with pe.Fori(0, NG) as g:
                pe.wait_ge(y_ready, g + 1)
                for b in range(NB):
                    for c in range(NC):
                        last = nc.tensor.matmul(tot_ps[64:128, b:b + 1], Z[:, b, c, 0:64], t["ones"][:, 0:1],
                                                start=(c == 0), stop=(c == NC - 1))
                last.then_inc(tot_ready, 1)
                for d4 in range(16):
                    pe.wait_ge(conv_out, g * 16 + d4 + 1)
                    for k in range(4):
                        d = d4 * 4 + k
                        nc.tensor.matmul(cps[d4 % 2][:, k, :, :], toep[:, d, :], Z[:, :, :, d], start=True, stop=True)
                        last = nc.tensor.matmul(cps[d4 % 2][0:64, k, :, 1:NC], toep_prev[64:128, d, :],
                                                Z[64:128, :, 0:NC - 1, d], start=False, stop=True, skip_group_check=True)
                    last.then_inc(conv_ready, 1)
                pe.wait_ge(filt_ready, g * 16 + 16)
                for b in range(NB):
                    n = g * NB + b

                    def turn(c4):
                        pe.wait_ge(zt_ready, n * 4 + c4 - 1 + 2)
                        for j in range(4):
                            last = nc.tensor.transpose(zp[c4 % 2][:, j, :], Z[:, b, c4 * 4 + j, :], t["ident"][:, :])
                        last.then_inc(z_ready, 1)

                    def product(c4):
                        pe.wait_ge(zt_ready, n * 4 + c4 + 1 + 2)
                        pe.wait_ge(o_out, n * 4 + c4 + 1)
                        nc.tensor.matmul(op[c4 % 2][:, :, :].rearrange("p c d -> p (c d)"), t["ones"][0:1, :], t["bias4"][:, :],
                                         start=True, stop=False)
                        for j in range(4):
                            last = nc.tensor.matmul(op[c4 % 2][:, j, :], zt[c4 % 2][:, j, :], t["w12"][:, :],
                                                    start=False, stop=(j == 3))
                        last.then_inc(o_ready, 1)

                    turn(0)
                    for c4 in range(1, 4):
                        turn(c4)
                        product(c4 - 1)
                    product(3)
                    if b == NB - 1:
                        pe.wait_ge(z_ready, n * 4 + 4)
                        pe.sem_inc(z_free, 1)
                    pe.wait_ge(y2_ready, n + 1)
                    for c4 in range(4):
                        pe.wait_ge(xp_out, n * 4 + c4 + 1)
                        pe.sem_inc(pace, 1)
                        for j in range(4):
                            last = nc.tensor.transpose(xp[:, j, :], y2[:, c4 * 4 + j, :], t["ident"][:, :])
                        last.then_inc(xp_ready, 1)
                    pe.wait_ge(xp_out, n * 4 + 5)
                    pe.wait_ge(gp_out, n + 1)
                    for c in range(NC):
                        last = nc.tensor.matmul(node_ps[:, c, :], xT[b % 2][:, c, :], t["w_cat"][:, :], start=True, stop=True)
                    last.then_inc(gp_ready, 1)

        @block.scalar
        def _(act):
            act.sem_inc(conv_out, 2)
            act.sem_inc(zt_ready, 2)
            act.sem_inc(xp_out, 1)
            with act.Fori(0, 2) as g2:
              for gb in range(2):
                g = g2 * 2 + gb
                for b in range(NB):
                    if b % 4 == 0:
                        act.wait_ge(h_in[gb][b // 4], (g2 + 1) * 64)
                    act.wait_ge(sq1_used, g * NB + b + 1)
                    act.activation(sq[:, :, :], H[gb][:, b, :, :], ACT.Square).then_inc(sq1, 1)
                act.wait_ge(var1, g + 1)
                act.activation(rs[:, :, :], tmp[:, :, :], ACT.Sqrt).then_inc(std1, 1)
                for d4 in range(16):
                    act.wait_ge(conv_ready, g * 16 + d4 + 1)
                    act.activation(Z[:, :, :, 64 + d4 * 4:68 + d4 * 4],
                                   cps[d4 % 2][:, :, :, :].rearrange("p k b c -> p b c k"), ACT.Copy).then_inc(filt_ready, 1)
                    act.wait_ge(filt_ready, g * 16 + d4 + 1)
                    act.sem_inc(conv_out, 1)
                act.wait_ge(zb_ready, g + 1)
                for b in range(NB):
                    n = g * NB + b
                    for c4 in range(4):
                        act.wait_ge(z_ready, n * 4 + c4 + 1)
                        act.wait_ge(o_ready, n * 4 + c4 - 2 + 1) if (c4 >= 2) else act.wait_ge(o_ready, n * 4)
                        act.activation(zt[c4 % 2][:, :, :], zp[c4 % 2][:, :, :], ACT.Identity, bias=zb[:, b:b + 1]).then_inc(zt_ready, 1)
                    act.wait_ge(h2_ready, n + 1)
                    act.wait_ge(sq1_used, (g + 1) * NB + 1)
                    act.activation(sq[:, :, :], H[gb][:, b, :, :], ACT.Square).then_inc(sq2, 1)
                    act.wait_ge(var2, n + 1)
                    act.activation(t4[:, :], t3[:, :], ACT.Sqrt).then_inc(std2, 1)
                    act.wait_ge(x_out[b % 2], (g * 4 + b // 2) * 16)
                    act.wait_ge(gp_ready, n)
                    for c4 in range(4):
                        act.wait_ge(xp_ready, n * 4 + c4 + 1)
                        act.activation(xT[b % 2][:, c4 * 4:c4 * 4 + 4, :], xp[:, :, :], ACT.Copy).then_inc(xp_out, 1)
                    act.wait_ge(xp_out, n * 4 + 5)
                    act.dma_start(dram["x3t"].rearrange("d (n t) -> d n t", t=2048)[:, bass.ds(n, 1), :].rearrange("d a t -> d (a t)"),
                                  shared[0:64, b % 2 * 2048:b % 2 * 2048 + 2048]).then_inc(x_out[b % 2], 16)

        @block.vector
        def _(v):
            v.sem_inc(sq1_used, 1)
            v.sem_inc(o_out, 2)
            v.sem_inc(gp_out, 1)
            ch = Chain(v, dve)
            K = 86
            nc.vector.memset(zb[0:64, :], 0.0)
            with v.Fori(0, 2) as g2:
              for gb in range(2):
                g = g2 * 2 + gb
                ch.start(g * K)
                for b in range(NB):
                    if b % 4 == 0:
                        v.wait_ge(h_in[gb][b // 4], (g2 + 1) * 64)
                    nc.vector.tensor_reduce(s1[:, b, :], H[gb][:, b, :, :], AX, ALU.add)
                    v.wait_ge(sq1, g * NB + b + 1)
                    nc.vector.tensor_reduce(s2[:, b, :], sq[:, :, :], AX, ALU.add).then_inc(sq1_used, 1)
                v.wait_ge(sq1_used, (g + 1) * NB + 1)
                ch.done(nc.vector.tensor_scalar(mean[:, :, :], s1[:, :, :], 1.0 / 64, None, ALU.mult))
                ch.done(nc.vector.tensor_tensor(tmp[:, :, :], mean[:, :, :], mean[:, :, :], ALU.mult))
                ch.done(nc.vector.scalar_tensor_tensor(tmp[:, :, :], s2[:, :, :], 1.0 / 64, tmp[:, :, :], ALU.mult, ALU.subtract))
                ch.done(nc.vector.tensor_scalar(tmp[:, :, :], tmp[:, :, :], 0.0, 1e-5, ALU.max, ALU.add))
                v.sem_inc(var1, 1)
                v.wait_ge(std1, g + 1)
                ch.done(nc.vector.reciprocal(rs[:, :, :], rs[:, :, :]))
                v.wait_ge(z_free, g + 1)
                for b in range(NB):
                    nc.vector.tensor_tensor(Z[:, b, :, 0:64], H[gb][:, b, :, :], bc(mean[:, b, :], 2, 64), ALU.subtract).then_inc(dve, 1)
                    ch.n += 1
                    if b:
                        v.wait_ge(dve, ch.base + ch.n - 1)
                        nc.vector.tensor_tensor(Z[:, b - 1, :, 0:64], Z[:, b - 1, :, 0:64], bc(rs[:, b - 1, :], 2, 64), ALU.mult)
                ch.done(nc.vector.tensor_scalar(t1[:, :], t["reset"][:, 0, 0:16], 0.0, None, ALU.mult))
                nc.vector.tensor_tensor(Z[:, 7, :, 0:64], Z[:, 7, :, 0:64], bc(rs[:, 7, :], 2, 64), ALU.mult).then_inc(y_ready, 1)
                v.wait_ge(tot_ready, g + 1)
                nc.vector.tensor_scalar(zb[64:128, :], tot_ps[64:128, :], t["m0"][64:128, :], None, ALU.mult).then_inc(zb_ready, 1)
                for b in range(NB):
                    n = g * NB + b
                    for c4 in range(4):
                        v.wait_ge(o_ready, n * 4 + c4 + 1)
                        nc.vector.tensor_tensor(H[gb][:, b, c4 * 4:c4 * 4 + 4, :], op[c4 % 2][:, :, :],
                                                H[gb][:, b, c4 * 4:c4 * 4 + 4, :], ALU.add).then_inc(o_out, 1)
                    v.wait_ge(o_out, n * 4 + 6)
                    v.sem_inc(h2_ready, 1)
                    hh = H[gb][:, b, :, :]
                    ch.done(nc.vector.tensor_reduce(t1[:, :], hh, AX, ALU.add))
                    ch.done(nc.vector.tensor_scalar(t1[:, :], t1[:, :], 1.0 / 64, None, ALU.mult))
                    ch.done(nc.vector.tensor_tensor(t2[:, :], t1[:, :], t1[:, :], ALU.mult))
                    v.wait_ge(sq2, n + 1)
                    ch.done(nc.vector.tensor_reduce(t3[:, :], sq[:, :, :], AX, ALU.add))
                    ch.done(nc.vector.scalar_tensor_tensor(t3[:, :], t3[:, :], 1.0 / 64, t2[:, :], ALU.mult, ALU.subtract))
                    ch.done(nc.vector.tensor_scalar(t3[:, :], t3[:, :], 0.0, 1e-5, ALU.max, ALU.add))
                    v.sem_inc(var2, 1)
                    v.wait_ge(xp_ready, n * 4)
                    ch.done(nc.vector.tensor_tensor(y2[:, :, :], hh, bc(t1[:, :], 2, 64), ALU.subtract))
                    v.wait_ge(std2, n + 1)
                    ch.done(nc.vector.reciprocal(t4[:, :], t4[:, :]))
                    nc.vector.tensor_tensor(y2[:, :, :], y2[:, :, :], bc(t4[:, :], 2, 64), ALU.mult).then_inc(y2_ready, 1)
                    v.wait_ge(y2_ready, n + 1)
                    v.wait_ge(node_out[b % 2], (g * 4 + b // 2) * 32)
                    v.wait_ge(gp_ready, n + 1)
                    ch.done(nc.vector.tensor_tensor(nrow[b % 2][:, :, :], node_ps, bc(t["unit"][:, :], 1, NC), ALU.add))
                    v.sem_inc(gp_out, 1)
                ch_n = ch.n
            assert ch_n == K, ch_n

        @block.gpsimd
        def _(pool):
            pool.sem_inc(h_free, 2)
            with pool.Fori(0, NG // 2) as g2:
                for gb in range(2):
                    g = g2 * 2 + gb
                    for b in range(NB):
                        n, s = g * NB + b, b % 2
                        pool.wait_ge(h2_ready, n + 1)
                        pool.dma_start(h2_rows[bass.ds(n, 1)].rearrange("a p c d -> (a p) c d"), H[gb][:, b, :, :]).then_inc(h2_out[s], 16)
                        pool.wait_ge(gp_out, n + 2)
                        pool.dma_start(node_rows[bass.ds(n, 1)].rearrange("a p c d -> (a p) c d"), nrow[s][:, :, :]).then_inc(node_out[s], 16)
                        pool.dma_start(node_own[bass.ds(n, 1)].rearrange("a p c d -> (a p) c d"), nrow[s][:, :, :]).then_inc(node_out[s], 16)
                    for s in range(2):
                        pool.wait_ge(h2_out[s], (g + 1) * 64)
                    pool.sem_inc(h_free, 1)
            for s in range(2):
                pool.wait_ge(h2_out[s], 256)
                pool.wait_ge(node_out[s], 512)
                pool.wait_ge(x_out[s], 256)


CHUNK = 128
CHUNKS = COLS // CHUNK
EARLY = 10
SLOTS = 8
ROW = 28


def busy_tiles(pool, t, move, sem, nothing):
    for g in range(NODE_TILES // SKIP_GROUP):
        some = pool.value_load(t["busy"][0:1, g:g + 1])
        with pool.If(some > 0):
            for c in range(g * SKIP_GROUP, (g + 1) * SKIP_GROUP):
                move(c).then_inc(sem, 16)
        with pool.Else():
            pool.dma_start(nothing[g:g + 1, :], t["busy"][0:1, 0:1]).then_inc(sem, 16 * SKIP_GROUP)


def pass_messages(nc, t, dram):
    edge_ad = dram["edge_ad"]
    runs = dram["runs"]
    with ExitStack() as ctx:
        sem = lambda n: ctx.enter_context(nc.semaphore(n))
        sb = lambda n, s, d=F32: ctx.enter_context(nc.sbuf_tensor(n, s, d))
        pt = lambda n, s: ctx.enter_context(nc.psum_tensor(n, s, F32))
        quarter = lambda i: t["edge_rows"][:, i * CHUNK * ROW:(i + 1) * CHUNK * ROW]
        E = [quarter(i).rearrange("p (f v) -> p f v", v=ROW) for i in range(2)]
        R = [quarter(2 + i).rearrange("p (f v) -> p f v", v=ROW) for i in range(2)]
        node_run = t["edge_rows"][:, :].rearrange("p (c v) -> p c v", v=ROW)
        dst = sb("m_dst", [128, COLS], U16)
        same = sb("same", [128, COLS])
        same_neg = sb("same_neg", [128, CHUNK])
        idx = [sb(f"src_row{i}", [128, CHUNK], I32) for i in range(2)]
        ad = [sb(f"ad{i}", [128, CHUNK, 4]) for i in range(2)]
        node_ad = sb("node_ad", [128, NODE_TILES, 4])
        score = sb("e_score", [128, CHUNK, 4])
        top = sb("top", [128, CHUNK + 1, 4])
        X = sb("X", [128, 2, CHUNK, 4])
        ad_last = sb("ad_last", [128, 4])
        sum_last = sb("sum_last", [128, 20])
        zeros = sb("zeros", [128, 1024])
        border = sb("border", [128, 2], U16)
        first_i = sb("first_i", [128, 2], I32)
        first_row = sb("first_row", [128, ROW])
        tail = sb("tail", [128, ROW])
        chain = sb("chain", [1, 128, ROW])
        chain_top = sb("chain_top", [1, 129, 4])
        chain_x = sb("chain_x", [1, 2, 128, 4])
        ends16 = sb("ends16", [1, 2, 128], U16)
        link = sb("link", [1, 3, 128])
        carry, patch = sb("carry", [128, ROW]), sb("patch", [128, ROW])
        px = sb("px", [128, 3, 4])
        place = sb("place", [128, 4])
        place_i = sb("place_i", [128, 2], I32)
        w1, w2 = sb("w1", [64, 4, 128]), sb("w2", [128, 4, 64])
        b1, b2 = sb("b1", [128, 4]), sb("b2", [128, 4, 64])
        xT = [sb(f"mxT{i}", [64, 2048]) for i in range(2)]
        hid = [sb(f"hid{i}", [128, 512]) for i in range(2)]
        ot = [sb(f"ot{i}", [128, 4, 16, 64]) for i in range(2)]
        IMAGE_COLS = COLS // 16
        PER_UNIT = IMAGE_COLS // 16
        digit = sb("digit", [128, IMAGE_COLS], U16)
        lo, hi = sb("c_lo", [128, IMAGE_COLS]), sb("c_hi", [128, IMAGE_COLS])
        num = sb("num", [128, 256], BF16)
        is_lo = [sb(f"is_lo{i}", [128, 256], BF16) for i in range(SLOTS)]
        is_hi = [sb(f"is_hi{i}", [128, 256], BF16) for i in range(SLOTS)]
        busy_f = sb("busy_f", [1, NODE_TILES // SKIP_GROUP])
        count, start, end, none = (t["edge_rows"][:, 2 * CHUNK * ROW + i * NODE_TILES:2 * CHUNK * ROW + (i + 1) * NODE_TILES]
                                   for i in range(4))
        hist, tps, bps = pt("hist", [128, 2, 256]), pt("total_ps", [128, 512]), pt("before_ps", [128, 512])
        num_ready, hot, hot_free, count_ready, summed, places_ready = (sem(n) for n in
            ("num_ready", "hot", "hot_free", "count_ready", "summed", "places_ready"))
        hp = [pt(f"hp{i}", [128, 512]) for i in range(2)]
        eo = [pt(f"eo{i}", [128, 4, 64]) for i in range(2)]
        (small_in, dst_in, zero_ready, zero_out, node_ad_in, first_in, ad_out, gat_free, x_ready,
         exp_ready, rows_ready, h_ready, g_ready, e_ready, eo_out, ot_done, tail_ready,
         carry_ready, place_ready, patch_in, patch_ready, patch_out, init_ready,
         dve, fin, tails_out, chain_in, carry_out, carry_in, first_ready, pace, pace_pool) = (sem(n) for n in (
         "m_small_in", "m_dst_in", "zero_ready", "zero_out", "node_ad_in", "first_in", "ad_out", "gat_free",
         "x_ready", "exp_ready", "rows_ready", "h_ready", "g_ready", "e_ready", "eo_out",
         "ot_done", "tail_ready", "carry_ready", "place_ready", "patch_in",
         "patch_ready", "patch_out", "init_ready", "m_dve", "m_fin", "tails_out", "chain_in",
         "carry_out", "carry_in", "first_ready", "m_pace", "m_pace_pool"))
        mx_in = [sem("mx_in0"), sem("mx_in1")]
        gathered = [sem("gathered0"), sem("gathered1")]
        idx_in = [sem("idx_in0"), sem("idx_in1")]
        spilled = [sem("spilled0"), sem("spilled1")]
        rows_in = [sem("rows_in0"), sem("rows_in1")]
        ad_in = [sem("ad_in0"), sem("ad_in1")]
        runs_out = [sem("runs_out0"), sem("runs_out1")]
        ot_out = [sem("ot_out0"), sem("ot_out1")]
        block = ctx.enter_context(nc.Block())
        row = lambda v: v.rearrange("(a n) -> a n", a=1)
        ad_c = edge_ad.rearrange("(p f) v -> p f v", p=128)
        runs_c = runs.rearrange("(p f) v -> p f v", p=128)
        experts = dram["experts"]

        @block.sync
        def _(sp):
            sp.dma_start(dst[:, :], dram["sorted_dst"]).then_inc(dst_in, 16)
            sp.dma_start(border[1:128, 0:1], dram["sorted_dst"][0:127, COLS - 1:COLS], allow_slow_non_contiguous=True).then_inc(dst_in, 16)
            src_rows = lambda k: dram["sorted_src"][:, bass.ds(k * CHUNK, CHUNK)]
            for s in range(2):
                sp.dma_start(idx[s][:, :], src_rows(s)).then_inc(idx_in[s], 16)
                sp.sem_inc(spilled[s], 16)
            sp.wait_ge(zero_ready, 1)
            flat = edge_ad.rearrange("(p f) v -> p (f v)", p=128)
            for k in range(8):
                sp.dma_start(flat[:, k * 1024:(k + 1) * 1024], zeros[:, :]).then_inc(zero_out, 16)
            sp.dma_start(node_ad[:, :, :], dram["node"].rearrange("(c p) v -> p c v", p=128)[:, :, 24:28]).then_inc(node_ad_in, 16)
            sp.dma_start(w1[:, :, :], dram["F_W1"].rearrange("e d f -> d e f")).then_inc(small_in, 16)
            sp.dma_start(w2[:, :, :], dram["F_W2"].rearrange("e f d -> f e d")).then_inc(small_in, 16)
            sp.dma_start(b1[:, :], dram["F_b1"].rearrange("e f -> f e"), allow_slow_non_contiguous=True).then_inc(small_in, 16)
            sp.dma_start(b2[:, :, :].rearrange("p e d -> p (e d)"),
                         row(dram["F_b2"].rearrange("e d -> (e d)")).to_broadcast([128, 256])).then_inc(small_in, 16)
            for k, c in enumerate((0, COLS - 1)):
                sp.dma_start(ends16[:, k, :], dram["sorted_dst"][:, c:c + 1].rearrange("p one -> one p"),
                             allow_slow_non_contiguous=True).then_inc(small_in, 16)

            def spill(k, k2, s, more=True):
                sp.wait_ge(gathered[s], (k2 + 1) * 16 * CHUNK)
                sp.dma_start(runs_c[:, bass.ds(k * CHUNK, CHUNK), :], E[s][:, :, :]).then_inc(spilled[s], 16)
                if more:
                    sp.dma_start(idx[s][:, :], src_rows(k + 2)).then_inc(idx_in[s], 16)

            def fetch(j):
                s = j % 2
                if j >= 2:
                    sp.wait_ge(gat_free, j - 1)
                    sp.wait_ge(runs_out[s], j // 2 * 16)
                sp.dma_start(ad[s][:, :, :], ad_c[:, j * CHUNK:(j + 1) * CHUNK, :]).then_inc(ad_in[s], 16)
                sp.wait_ge(spilled[s], (j // 2 + 2) * 16)
                sp.dma_start(R[s][:, :, :], runs_c[:, j * CHUNK:(j + 1) * CHUNK, :]).then_inc(rows_in[s], 16)

            def store(j):
                sp.wait_ge(rows_ready, j + 1)
                sp.dma_start(runs_c[:, j * CHUNK:(j + 1) * CHUNK, :], R[j % 2][:, :, :]).then_inc(runs_out[j % 2], 16)

            with sp.Fori(0, EARLY // 2) as k2:
                for s in range(2):
                    spill(k2 * 2 + s, k2, s)
            sp.wait_ge(ad_out, 16 * NODE_TILES)
            spill_before = {2: EARLY, 5: EARLY + 1, 8: EARLY + 2, 10: EARLY + 3, 12: EARLY + 4}
            fetch(0)
            for j in range(CHUNKS - 1):
                if j in spill_before:
                    k = spill_before[j]
                    spill(k, k // 2, k % 2, k + 2 < CHUNKS)
                if j < CHUNKS - 2:
                    fetch(j + 1)
                store(j)
            spill(CHUNKS - 1, CHUNKS // 2 - 1, 1, False)
            fetch(CHUNKS - 1)
            store(CHUNKS - 1)
            sp.wait_ge(tail_ready, 1)
            sp.dma_start(dram["tails"], tail[:, :]).then_inc(tails_out, 16)
            sp.wait_ge(tails_out, 16)
            sp.dma_start(chain[:, :, :].rearrange("a p v -> a (p v)"), row(dram["tails"].rearrange("p v -> (p v)"))).then_inc(chain_in, 16)
            sp.wait_ge(carry_ready, 1)
            sp.dma_start(row(dram["carries"].rearrange("p v -> (p v)")), chain[:, :, :].rearrange("a p v -> a (p v)")).then_inc(carry_out, 16)
            sp.wait_ge(carry_out, 16)
            sp.dma_start(carry[1:128, :], dram["carries"][0:127, :]).then_inc(carry_in, 16)
            for s in range(2):
                sp.wait_ge(runs_out[s], CHUNKS * 8)

        @block.gpsimd
        def _(pool):
            nc.gpsimd.iota(place_i[:, 0:1], pattern=[[0, 1]], base=0, channel_multiplier=COLS).then_inc(place_ready, 1)
            nc.gpsimd.iota(num[:, :], pattern=[[1, 256]], base=0, channel_multiplier=0,
                           allow_small_or_imprecise_dtypes=True).then_inc(num_ready, 1)
            pool.wait_ge(first_ready, 1)
            pool.indirect_dma_start(out=first_row[:, :], out_offset=None, in_=dram["node"],
                                    in_offset=bass.IndirectOffsetOnAxis(ap=first_i[:, 0:1], axis=0)).then_inc(first_in, 16)

            def gather(first, last):
                with pool.Fori(first // 2, last // 2) as k2:
                    for s in range(2):
                        pool.wait_ge(idx_in[s], (k2 + 1) * 16)
                        pool.wait_ge(spilled[s], (k2 + 1) * 16)
                        pool.sem_inc(pace_pool, 1)
                        for f in range(CHUNK):
                            pool.indirect_dma_start(out=E[s][:, f, :], out_offset=None, in_=dram["node"],
                                                    in_offset=bass.IndirectOffsetOnAxis(ap=idx[s][:, f:f + 1], axis=0)
                                                    ).then_inc(gathered[s], 16)

            gather(0, EARLY)
            pool.wait_ge(zero_out, 128)
            pool.wait_ge(node_ad_in, 16)
            pool.wait_ge(places_ready, 1)
            pool.sem_inc(pace_pool, 1)
            busy_tiles(pool, t, lambda c: pool.indirect_dma_start(
                out=edge_ad, out_offset=bass.IndirectOffsetOnAxis(ap=t["first_edge"][:, c:c + 1], axis=0),
                in_=node_ad[:, c, :], in_offset=None, bounds_check=N_EDGES - 1, oob_is_err=False), ad_out, dram["nothing"][0])
            gather(EARLY, CHUNKS)
            pool.wait_ge(place_ready, 3)
            for s in range(2):
                pool.wait_ge(runs_out[s], CHUNKS * 8)
            at = bass.IndirectOffsetOnAxis(ap=place_i[:, 1:2], axis=0)
            pool.indirect_dma_start(out=patch[:, :], out_offset=None, in_=runs, in_offset=at,
                                    bounds_check=N_EDGES - 1, oob_is_err=False).then_inc(patch_in, 16)
            pool.wait_ge(patch_ready, 1)
            pool.indirect_dma_start(out=runs, out_offset=at, in_=patch[:, :], in_offset=None,
                                    bounds_check=N_EDGES - 1, oob_is_err=False).then_inc(patch_out, 16)
            pool.wait_ge(patch_out, 16)
            pool.wait_ge(init_ready, 1)
            busy_tiles(pool, t, lambda c: pool.indirect_dma_start(
                out=node_run[:, c, :], out_offset=None, in_=runs,
                in_offset=bass.IndirectOffsetOnAxis(ap=t["last_edge"][:, c:c + 1], axis=0),
                bounds_check=N_EDGES - 1, oob_is_err=False), fin, dram["nothing"][1])
            pool.wait_ge(fin, 16 * NODE_TILES)

        @block.tensor
        def _(pe):
            pe.wait_ge(small_in, 16 * 6)
            pe.sem_inc(e_ready, 16)
            pe.wait_ge(num_ready, 3)
            for half in range(2):
                last = nc.tensor.matmul(hist[:, half, :], is_lo[0][:, 0:128], is_hi[0][:, :], start=(half == 0), stop=True,
                                        skip_group_check=True)
            last.then_inc(hot_free, SLOTS)

            def add_counts(n, u):
                for c in range(u * PER_UNIT, (u + 1) * PER_UNIT):
                    s = c % SLOTS
                    pe.wait_ge(hot, n * IMAGE_COLS + c + 1)
                    for half in range(2):
                        last = nc.tensor.matmul(hist[:, half, :], is_lo[s][:, half * 128:half * 128 + 128], is_hi[s][:, :],
                                                start=False, stop=True, skip_group_check=True)
                    last.then_inc(hot_free, 1)

            def experts_of(i2, m, counting):
                n = i2 * 2 + m
                pe.wait_ge(mx_in[m], (i2 + 1) * 16)

                def second(u):
                    pe.wait_ge(g_ready, n * 16 + u + 1)
                    pe.wait_ge(eo_out, n * 16 + u + 1)
                    for j in range(4):
                        last = nc.tensor.matmul(eo[u % 2][:, j, :], hid[u % 2][:, j * 128:(j + 1) * 128], w2[:, u % 4, :],
                                                start=True, stop=True)
                    last.then_inc(e_ready, 1)

                for u in range(16):
                    if u > 1:
                        pe.wait_ge(g_ready, n * 16 + u - 1)
                    nc.tensor.matmul(hp[u % 2][:, :], w1[:, u % 4, :], xT[m][:, (u // 4) * 512:(u // 4) * 512 + 512],
                                     start=True, stop=True).then_inc(h_ready, 1)
                    if u:
                        second(u - 1)
                    if counting:
                        add_counts(n, u)
                second(15)

            with pe.Fori(0, 8) as i2:
                for m in range(2):
                    experts_of(i2, m, True)
            pe.wait_ge(hot_free, COLS + SLOTS)
            pe.sem_inc(summed, 1)
            pe.wait_ge(count_ready, 1)
            nc.tensor.matmul(tps[:, :], t["ones"][:, :], count, start=True, stop=True).then_inc(summed, 1)
            nc.tensor.matmul(bps[:, :], t["before"][:, :], count, start=True, stop=True).then_inc(summed, 1)
            with pe.Fori(8, 16) as i2:
                for m in range(2):
                    experts_of(i2, m, False)

        @block.scalar
        def _(act):
            for m in range(2):
                act.sem_inc(ot_out[m], 16)

            def experts_of(n, m):
                if m == 0:
                    for i in range(2):
                        act.dma_start(xT[i][:, :], dram["x3t"].rearrange("d (n t) -> d n t", t=2048)[:, bass.ds(n + i, 1), :]
                                      .rearrange("d a t -> d (a t)")).then_inc(mx_in[i], 16)
                for u in range(16):
                    act.wait_ge(h_ready, n * 16 + u + 1)
                    act.wait_ge(e_ready, n * 16 + u + 15)
                    act.activation(hid[u % 2][:, :], hp[u % 2][:, :], ACT.Gelu, bias=b1[:, u % 4:u % 4 + 1]).then_inc(g_ready, 1)
                act.wait_ge(ot_done, n + 1)
                act.dma_start(experts[bass.ds(n, 1)].rearrange("a p v -> (a p) v"),
                              ot[m][:, :, :, :].rearrange("p e c d -> p (e c d)")).then_inc(ot_out[m], 16)

            with act.Fori(0, 12) as i2:
                for m in range(2):
                    experts_of(i2 * 2 + m, m)
            with act.Fori(0, CHUNKS // 4) as k4:
                for m, s in ((0, 0), (0, 1), (1, 0), (1, 1)):
                    if s == 0:
                        experts_of(k4 * 2 + m + 24, m)
                    act.wait_ge(x_ready, k4 * 4 + m * 2 + s + 1)
                    act.activation(X[:, :, :, :], X[:, :, :, :], ACT.Exp).then_inc(exp_ready, 1)
            for m in range(2):
                act.wait_ge(ot_out[m], 17 * 16)
            act.wait_ge(x_ready, CHUNKS + 1)
            act.activation(chain_x[:, :, :, :], chain_x[:, :, :, :], ACT.Exp).then_inc(exp_ready, 1)
            act.wait_ge(x_ready, CHUNKS + 2)
            act.activation(px[:, 1:3, :], px[:, 1:3, :], ACT.Exp).then_inc(exp_ready, 1)

        @block.vector
        def _(v):
            ch = Chain(v, dve)
            v.sem_inc(eo_out, 2)
            nc.vector.memset(zeros[:, :], 0.0).then_inc(zero_ready, 1)
            ch.done(nc.vector.memset(sum_last[:, :], 0.0))
            ch.done(nc.vector.memset(top[:, 0:1, :], LOW))
            ch.done(nc.vector.memset(tail[:, :], 0.0))
            ch.done(nc.vector.memset(carry[:, :], 0.0))
            ch.done(nc.vector.memset(patch[:, :], 0.0))
            ch.done(nc.vector.memset(place[:, :], 0.0))
            nc.vector.memset(is_lo[0][:, :], 0.0).then_inc(num_ready, 1)
            nc.vector.memset(is_hi[0][:, :], 0.0).then_inc(num_ready, 1)
            ch.done(nc.vector.memset(border[0:1, 0:1], 0))
            v.wait_ge(dst_in, 32)
            ch.done(nc.vector.tensor_copy(first_i[:, 0:1], dst[:, 0:1]))
            v.sem_inc(first_ready, 1)
            nc.vector.tensor_tensor(same[:, 1:COLS], dst[:, 1:COLS], dst[:, 0:COLS - 1], ALU.is_equal)
            ch.done(nc.vector.tensor_tensor(same[:, 0:1], dst[:, 0:1], border[:, 0:1], ALU.is_equal))
            ch.done(nc.vector.memset(same[0:1, 0:1], 0.0))
            v.wait_ge(first_in, 16)
            ch.done(nc.vector.tensor_copy(ad_last[:, :], first_row[:, 24:28]))
            v.wait_ge(small_in, 96)
            v.wait_ge(num_ready, 3)
            base = ch.n

            def segment_run(rows, high, score_t, neg_t, x, sum_before, asked, answered, answers):
                F = rows.shape[1]
                now, before = high[:, 1:F + 1, :], high[:, 0:F, :]
                for h in range(4):
                    last = nc.vector.tensor_tensor_scan(high[:, 1:F + 1, h], neg_t, score_t[:, :, h], high[:, 0:1, h],
                                                        ALU.add, ALU.max)
                ch.done(last)
                nc.vector.tensor_tensor(x[:, 1, :, :], score_t, now, ALU.subtract)
                ch.done(nc.vector.tensor_tensor(x[:, 0, :, :], before, bc(neg_t, 2, 4), ALU.add))
                ch.done(nc.vector.tensor_tensor(x[:, 0, :, :], x[:, 0, :, :], now, ALU.subtract))
                v.sem_inc(asked, 1)
                v.wait_ge(answered, answers)
                sums = rows[:, :, 0:20].rearrange("p f (h v) -> p f h v", v=5)
                ch.done(nc.vector.tensor_tensor(sums, sums, bc(x[:, 1, :, :], 3, 5), ALU.mult))
                for c in range(20):
                    last = nc.vector.tensor_tensor_scan(rows[:, :, c], x[:, 0, :, c // 5], rows[:, :, c], sum_before(c), ALU.mult, ALU.add)
                ch.done(last)
                ch.done(nc.vector.tensor_copy(rows[:, :, 20:24], now))

            def one_hots(n, u):
                for c in range(u * PER_UNIT, (u + 1) * PER_UNIT):
                    s = c % SLOTS
                    v.wait_ge(hot_free, n * IMAGE_COLS + c + 1)
                    nc.vector.tensor_scalar(is_lo[s][:, :], num[:, :], lo[:, c:c + 1], None, ALU.is_equal)
                    nc.vector.tensor_scalar(is_hi[s][:, :], num[:, :], hi[:, c:c + 1], None, ALU.is_equal).then_inc(hot, 1)

            def experts_of(n, m, free, counting):
                v.wait_ge(ot_out[m], free)

                def add_bias(u):
                    v.wait_ge(e_ready, n * 16 + u + 17)
                    c0 = u // 4 * 4
                    nc.vector.tensor_tensor(ot[m][:, u % 4, c0:c0 + 4, :], eo[u % 2][:, :, :],
                                            bc(b2[:, u % 4, :], 1, 4), ALU.add).then_inc(eo_out, 1)

                for u in range(16):
                    if counting:
                        one_hots(n, u)
                    if u:
                        add_bias(u - 1)
                add_bias(15)
                v.wait_ge(eo_out, n * 16 + 18)
                v.sem_inc(ot_done, 1)

            with v.Fori(0, 8) as i2:
                for m in range(2):
                    n = i2 * 2 + m
                    ch.start(base + n * 4)
                    part = dst[:, bass.ds(n * IMAGE_COLS, IMAGE_COLS)]
                    for split, amount, digits in ((ALU.bitwise_and, 255, lo), (ALU.logical_shift_right, 8, hi)):
                        ch.done(nc.vector.tensor_scalar(digit[:, :], part, amount, None, split))
                        ch.done(nc.vector.tensor_copy(digits[:, :], digit[:, :]))
                    experts_of(n, m, (i2 + 1) * 16, True)
            ch.start(base + 16 * 4)
            v.wait_ge(summed, 1)
            ch.done(nc.vector.tensor_copy(count.rearrange("p (n k) -> p k n", k=2), hist[:, :, :]))
            v.sem_inc(count_ready, 1)
            v.wait_ge(summed, 3)
            ch.done(nc.vector.memset(none, 1.0))
            ch.done(nc.vector.tensor_copy(end, tps[:, :]))
            ch.done(nc.vector.tensor_tensor_scan(start, none, end, 0.0, ALU.mult, ALU.add))
            ch.done(nc.vector.tensor_tensor(start, start, end, ALU.subtract))
            ch.done(nc.vector.tensor_reduce(busy_f[:, :], end[0:1, :].rearrange("a (g c) -> a g c", c=SKIP_GROUP), AX, ALU.add))
            ch.done(nc.vector.tensor_copy(t["busy"][:, :], busy_f[:, :]))
            ch.done(nc.vector.tensor_copy(end, bps[:, :]))
            ch.done(nc.vector.tensor_tensor(start, start, end, ALU.add))
            ch.done(nc.vector.scalar_tensor_tensor(end, start, -1.0, count, ALU.add, ALU.add))
            ch.done(nc.vector.tensor_scalar(none, count, 0.5, float(SKIP), ALU.is_lt, ALU.mult))
            ch.done(nc.vector.tensor_tensor(start, start, none, ALU.max))
            ch.done(nc.vector.tensor_tensor(end, end, none, ALU.max))
            ch.done(nc.vector.tensor_copy(t["first_edge"][:, :], start))
            ch.done(nc.vector.tensor_copy(t["last_edge"][:, :], end))
            v.sem_inc(places_ready, 1)
            base += 16 * 4 + ch.n
            with v.Fori(8, 12) as i2:
                for m in range(2):
                    experts_of(i2 * 2 + m, m, (i2 + 1) * 16, False)

            K = 13
            with v.Fori(0, CHUNKS // 4) as k4:
                for m, s in ((0, 0), (0, 1), (1, 0), (1, 1)):
                    k2 = k4 * 2 + m
                    k = k2 * 2 + s
                    if s == 0:
                        experts_of(k2 + 24, m, (k4 + 13) * 16, False)
                    ch.start(base + k * K)
                    v.wait_ge(ad_in[s], (k2 + 1) * 16)
                    v.sem_inc(pace, 1)
                    here = same[:, bass.ds(k * CHUNK, CHUNK)]
                    for h in range(4):
                        last = nc.vector.tensor_tensor_scan(ad[s][:, :, h], here, ad[s][:, :, h], ad_last[:, h:h + 1], ALU.mult, ALU.add)
                    ch.done(last)
                    ch.done(nc.vector.tensor_copy(ad_last[:, :], ad[s][:, CHUNK - 1, :]))
                    ch.done(nc.vector.tensor_scalar(same_neg[:, :], here, -1.0, -LOW, ALU.add, ALU.mult))
                    v.wait_ge(rows_in[s], (k2 + 1) * 16)
                    ch.done(nc.vector.tensor_tensor(score[:, :, :], R[s][:, :, 20:24], ad[s][:, :, :], ALU.add))
                    ch.done(nc.vector.scalar_tensor_tensor(score[:, :, :], score[:, :, :], 0.2, score[:, :, :], ALU.mult, ALU.max))
                    v.sem_inc(gat_free, 1)
                    segment_run(R[s], top, score[:, :, :], same_neg[:, :], X, lambda c: sum_last[:, c:c + 1],
                                x_ready, exp_ready, k + 1)
                    ch.done(nc.vector.tensor_copy(top[:, 0:1, :], top[:, CHUNK:CHUNK + 1, :]))
                    ch.done(nc.vector.tensor_copy(sum_last[:, :], R[s][:, CHUNK - 1, 0:20]))
                    v.sem_inc(rows_ready, 1)
                    k_used = ch.n
            assert k_used == K, k_used
            ch.start(base + CHUNKS * K)
            nc.vector.tensor_copy(tail[:, 0:20], sum_last[:, :])
            ch.done(nc.vector.tensor_copy(tail[:, 20:24], top[:, 0, :]))
            v.sem_inc(tail_ready, 1)
            v.wait_ge(place_ready, 1)
            ch.done(nc.vector.tensor_copy(place[:, 0:1], dst[:, 0:1]))
            is_first = node_ad[:, :, :].rearrange("p c h -> p (c h)")
            ch.done(nc.vector.tensor_scalar(is_first, dst[:, :], place[:, 0:1], None, ALU.is_equal))
            ch.done(nc.vector.tensor_reduce(place[:, 1:2], is_first, AX, ALU.add))
            ch.done(nc.vector.tensor_copy(place[:, 2:3], place_i[:, 0:1]))
            ch.done(nc.vector.tensor_scalar(place[:, 1:2], place[:, 1:2], place[:, 2:3], -1.0 - SKIP, ALU.add, ALU.add))
            ch.done(nc.vector.tensor_scalar(place[:, 1:2], place[:, 1:2], same[:, 0:1], float(SKIP), ALU.mult, ALU.add))
            ch.done(nc.vector.tensor_copy(place_i[:, 1:2], place[:, 1:2]))
            v.sem_inc(place_ready, 2)
            ch.done(nc.vector.memset(chain_top[:, 0:1, :], LOW))
            ch.done(nc.vector.memset(link[:, 0, 0:1], 0.0))
            ch.done(nc.vector.tensor_tensor(link[:, 0, 1:128], ends16[:, 0, 1:128], ends16[:, 1, 0:127], ALU.is_equal))
            ch.done(nc.vector.tensor_tensor(link[:, 1, :], ends16[:, 0, :], ends16[:, 1, :], ALU.is_equal))
            ch.done(nc.vector.tensor_tensor(link[:, 0, :], link[:, 0, :], link[:, 1, :], ALU.mult))
            ch.done(nc.vector.tensor_scalar(link[:, 2, :], link[:, 0, :], -1.0, -LOW, ALU.add, ALU.mult))
            v.wait_ge(chain_in, 16)
            segment_run(chain[:, :, :], chain_top, chain[:, :, 20:24], link[:, 2, :], chain_x, lambda c: 0.0,
                        x_ready, exp_ready, CHUNKS + 1)
            v.sem_inc(carry_ready, 1)
            for s in range(2):
                v.wait_ge(runs_out[s], CHUNKS * 8)
            ch.done(nc.vector.memset(t["edge_rows"][:, :], 0.0))
            ch.done(nc.vector.memset(node_run[:, :, 20:24], LOW))
            v.sem_inc(init_ready, 1)
            v.wait_ge(carry_in, 16)
            v.wait_ge(patch_in, 16)
            ch.done(nc.vector.tensor_tensor(px[:, 0, :], patch[:, 20:24], carry[:, 20:24], ALU.max))
            nc.vector.tensor_tensor(px[:, 1, :], patch[:, 20:24], px[:, 0, :], ALU.subtract)
            ch.done(nc.vector.tensor_tensor(px[:, 2, :], carry[:, 20:24], px[:, 0, :], ALU.subtract))
            v.sem_inc(x_ready, 1)
            v.wait_ge(exp_ready, CHUNKS + 2)
            for k, tile in ((1, patch), (2, carry)):
                sums = tile[:, 0:20].rearrange("p (h v) -> p h v", v=5)
                ch.done(nc.vector.tensor_tensor(sums, sums, bc(px[:, k, :], 2, 5), ALU.mult))
            ch.done(nc.vector.tensor_tensor(patch[:, 0:20], patch[:, 0:20], carry[:, 0:20], ALU.add))
            ch.done(nc.vector.tensor_copy(patch[:, 20:24], px[:, 0, :]))
            v.sem_inc(patch_ready, 1)


def combine(nc, t, dram):
    node_run = t["edge_rows"][:, :].rearrange("p (c v) -> p c v", v=ROW)
    C = 64
    out_rows = dram["out"].rearrange("b (c p) d -> b p c d", p=128)
    with ExitStack() as ctx:
        sem = lambda n: ctx.enter_context(nc.semaphore(n))
        sb = lambda n, s, d=F32: ctx.enter_context(nc.sbuf_tensor(n, s, d))
        nd = [sb(f"nd{i}", [128, C, ROW]) for i in range(2)]
        X = sb("rx", [128, 2, C, 4])
        own, high = sb("own", [128, C, 4]), sb("high", [128, C, 4])
        agg, agg2 = sb("agg", [128, C, 16]), sb("agg2", [128, C, 16])
        den = sb("den", [128, C, 4])
        m1, m2 = sb("m1", [128, C]), sb("m2", [128, C])
        sc, sel = sb("r_score", [128, C, 4]), sb("r_sel", [128, C, 4])
        beats = sb("beats", [128, C, 4, 3])
        gate = sb("gate", [128, NODE_TILES, 4])
        const = sb("r_const", [128, 3, 16])
        PER = 4
        ex = [sb(f"ex{i}", [128, 4, 16, 64]) for i in range(PER)]
        hb = [sb(f"hb{i}", [128, 16, 64]) for i in range(PER)]
        out_done = [sem(f"out_done{i}") for i in range(PER)]
        const_in, dve, x_ready, exp_ready, std_ready, var_ready, nd_free, ex_free, pool_done, prod_ready, sum_ready = (
            sem(n) for n in ("const_in", "r_dve", "rx_ready", "rexp_ready", "rstd_ready", "rvar_ready", "nd_free",
                             "ex_free", "pool_done", "prod_ready", "sum_ready"))
        half_ready, pair_ready, gates_ready = sem("half_ready"), sem("pair_ready"), sem("gates_ready")
        nd_in = [sem("nd_in0"), sem("nd_in1")]
        ex_in = [sem(f"ex_in{i}") for i in range(PER)]
        third_ready = sem("third_ready")
        block = ctx.enter_context(nc.Block())
        G = NODE_TILES // C

        @block.sync
        def _(sp):
            for k, name in enumerate(("b_gat", "ln_gamma", "ln_beta")):
                sp.dma_start(const[:, k, :], dram[name].rearrange("(a n) -> a n", a=1).to_broadcast([128, 16])).then_inc(const_in, 16)
            with sp.Fori(0, G // 2) as k2:
                for kb in range(2):
                    k = k2 * 2 + kb
                    sp.wait_ge(nd_free, k + 1)
                    sp.dma_start(nd[kb][:, :, :].rearrange("p (b c) v -> p b (c v)", b=4),
                                 dram["node_own"][bass.ds(k * 4, 4)].rearrange("b p c v -> p b (c v)")).then_inc(nd_in[kb], 16)
                    for s in range(PER):
                        n = k * PER + s
                        sp.wait_ge(ex_free, n + 1)
                        sp.dma_start(ex[s][:, :, :, :].rearrange("p e c d -> p (e c d)"),
                                     dram["experts"][bass.ds(n, 1)].rearrange("a p v -> (a p) v")).then_inc(ex_in[s], 16)
                        sp.wait_ge(out_done[s], k * 16 + 16)
                        sp.dma_start(hb[s][:, :, :].rearrange("p c d -> p (c d)"),
                                     dram["h2"][bass.ds(n, 1)].rearrange("a p c d -> (a p) (c d)")).then_inc(ex_in[s], 16)

        @block.scalar
        def _(act):
            for s in range(PER):
                act.sem_inc(out_done[s], 16)
            with act.Fori(0, G) as k:
                act.wait_ge(x_ready, 2 * k + 1)
                act.activation(X[:, :, :, :], X[:, :, :, :], ACT.Exp).then_inc(exp_ready, 1)
                act.wait_ge(var_ready, k + 1)
                act.activation(m1[:, :], m2[:, :], ACT.Sqrt).then_inc(std_ready, 1)
                act.wait_ge(x_ready, 2 * k + 2)
                act.activation(X[:, 0, :, :], X[:, 0, :, :], ACT.Exp).then_inc(exp_ready, 1)
                for s in range(PER):
                    n = k * PER + s
                    act.wait_ge(sum_ready, n + 1)
                    act.dma_start(out_rows[bass.ds(n, 1)].rearrange("a p c d -> (a p) c d"), hb[s][:, :, :]).then_inc(out_done[s], 16)
            for s in range(PER):
                act.wait_ge(out_done[s], 16 + G * 16)

        @block.gpsimd
        def _(pool):
            with pool.Fori(0, G) as k:
                for s in range(PER):
                    n = k * PER + s
                    pool.wait_ge(gates_ready, k + 1)
                    pool.wait_ge(ex_in[s], (k + 1) * 32)
                    nc.gpsimd.tensor_tensor(ex[s][:, 3, :, :], ex[s][:, 3, :, :], bc(gate[:, bass.ds(n * 16, 16), 3], 2, 64),
                                            ALU.mult).then_inc(third_ready, 1)
                    pool.wait_ge(prod_ready, n + 1)
                    nc.gpsimd.tensor_tensor(ex[s][:, 0, :, :], ex[s][:, 0, :, :], ex[s][:, 1, :, :], ALU.add).then_inc(pool_done, 1)
                    pool.wait_ge(pool_done, n + 1)
                    pool.wait_ge(half_ready, n + 1)
                    nc.gpsimd.tensor_tensor(hb[s][:, :, :], hb[s][:, :, :], ex[s][:, 0, :, :], ALU.add).then_inc(sum_ready, 1)
                    pool.wait_ge(sum_ready, n + 1)
                    pool.sem_inc(ex_free, 1)

        @block.vector
        def _(v):
            ch = Chain(v, dve)
            v.sem_inc(nd_free, 2)
            v.sem_inc(ex_free, PER)
            v.wait_ge(const_in, 48)
            wide = lambda k: bc(const[:, k, :], 1, C)
            flat16 = lambda a: a[:, :, :]
            K = 31
            with v.Fori(0, G // 2) as k2:
                for s in range(2):
                    k = k2 * 2 + s
                    ch.start(k * K)
                    v.wait_ge(nd_in[s], (k2 + 1) * 16)
                    here = node_run[:, bass.ds(k * C, C), :]
                    ch.done(nc.vector.tensor_tensor(own[:, :, :], nd[s][:, :, 20:24], nd[s][:, :, 24:28], ALU.add))
                    ch.done(nc.vector.scalar_tensor_tensor(own[:, :, :], own[:, :, :], 0.2, own[:, :, :], ALU.mult, ALU.max))
                    ch.done(nc.vector.tensor_tensor(high[:, :, :], own[:, :, :], here[:, :, 20:24], ALU.max))
                    nc.vector.tensor_tensor(X[:, 0, :, :], own[:, :, :], high[:, :, :], ALU.subtract)
                    ch.done(nc.vector.tensor_tensor(X[:, 1, :, :], here[:, :, 20:24], high[:, :, :], ALU.subtract))
                    v.sem_inc(x_ready, 1)
                    v.wait_ge(exp_ready, 2 * k + 1)
                    a = nd[s][:, :, 0:20].rearrange("p c (h v) -> p c h v", v=5)
                    b = here[:, :, 0:20].rearrange("p c (h v) -> p c h v", v=5)
                    nc.vector.tensor_tensor(a, a, bc(X[:, 0, :, :], 3, 5), ALU.mult)
                    ch.done(nc.vector.tensor_tensor(b, b, bc(X[:, 1, :, :], 3, 5), ALU.mult))
                    ch.done(nc.vector.tensor_tensor(a, a, b, ALU.add))
                    ch.done(nc.vector.tensor_scalar(den[:, :, :], a[:, :, :, 0], 1e-16, None, ALU.add))
                    ch.done(nc.vector.reciprocal(den[:, :, :], den[:, :, :]))
                    g4 = agg[:, :, :].rearrange("p c (h v) -> p c h v", v=4)
                    ch.done(nc.vector.tensor_tensor(g4, a[:, :, :, 1:5], bc(den[:, :, :], 3, 4), ALU.mult))
                    v.sem_inc(nd_free, 1)
                    ch.done(nc.vector.tensor_tensor(agg[:, :, :], agg[:, :, :], wide(0), ALU.add))
                    ch.done(nc.vector.tensor_reduce(m1[:, :], agg[:, :, :], AX, ALU.add))
                    ch.done(nc.vector.tensor_scalar(m1[:, :], m1[:, :], 1.0 / 16, None, ALU.mult))
                    ch.done(nc.vector.tensor_tensor(agg[:, :, :], agg[:, :, :], bc(m1[:, :], 2, 16), ALU.subtract))
                    ch.done(nc.vector.tensor_tensor(agg2[:, :, :], agg[:, :, :], agg[:, :, :], ALU.mult))
                    ch.done(nc.vector.tensor_reduce(m2[:, :], agg2[:, :, :], AX, ALU.add))
                    ch.done(nc.vector.tensor_scalar(m2[:, :], m2[:, :], 1.0 / 16, 1e-5, ALU.mult, ALU.add))
                    v.sem_inc(var_ready, 1)
                    v.wait_ge(std_ready, k + 1)
                    ch.done(nc.vector.reciprocal(m1[:, :], m1[:, :]))
                    ch.done(nc.vector.tensor_tensor(agg[:, :, :], agg[:, :, :], bc(m1[:, :], 2, 16), ALU.mult))
                    ch.done(nc.vector.tensor_tensor(agg[:, :, :], agg[:, :, :], wide(1), ALU.mult))
                    ch.done(nc.vector.tensor_tensor(agg[:, :, :], agg[:, :, :], wide(2), ALU.add))
                    ch.done(nc.vector.tensor_reduce(sc[:, :, :], agg[:, :, :].rearrange("p c (h v) -> p c v h", v=4), AX, ALU.add))
                    ch.done(nc.vector.tensor_scalar(sc[:, :, :], sc[:, :, :], 0.25, None, ALU.mult))
                    for e in range(4):
                        for q, o in enumerate(x for x in range(4) if x != e):
                            last = nc.vector.tensor_tensor(beats[:, :, e, q], sc[:, :, o], sc[:, :, e], ALU.is_ge if o < e else ALU.is_gt)
                    ch.done(last)
                    ch.done(nc.vector.tensor_reduce(sel[:, :, :], beats[:, :, :, :], AX, ALU.add))
                    ch.done(nc.vector.tensor_scalar(sel[:, :, :], sel[:, :, :], 1.5, None, ALU.is_lt))
                    ch.done(nc.vector.tensor_reduce(m1[:, :], sc[:, :, :], AX, ALU.max))
                    ch.done(nc.vector.tensor_tensor(X[:, 0, :, :], sc[:, :, :], bc(m1[:, :], 2, 4), ALU.subtract))
                    v.sem_inc(x_ready, 1)
                    v.wait_ge(exp_ready, 2 * k + 2)
                    ch.done(nc.vector.tensor_tensor(sel[:, :, :], sel[:, :, :], X[:, 0, :, :], ALU.mult))
                    ch.done(nc.vector.tensor_reduce(m1[:, :], sel[:, :, :], AX, ALU.add))
                    ch.done(nc.vector.reciprocal(m1[:, :], m1[:, :]))
                    ch.done(nc.vector.tensor_tensor(gate[:, bass.ds(k * C, C), :], sel[:, :, :], bc(m1[:, :], 2, 4), ALU.mult))
                    k_used = ch.n
                    v.sem_inc(gates_ready, 1)
                    for s in range(PER):
                        n = k * PER + s
                        v.wait_ge(ex_in[s], (k + 1) * 32)
                        gates = gate[:, bass.ds(n * 16, 16), :]
                        nc.vector.tensor_tensor(ex[s][:, 0, :, :], ex[s][:, 0, :, :], bc(gates[:, :, 0], 2, 64), ALU.mult)
                        nc.vector.tensor_tensor(ex[s][:, 1, :, :], ex[s][:, 1, :, :], bc(gates[:, :, 1], 2, 64), ALU.mult).then_inc(prod_ready, 1)
                        nc.vector.tensor_tensor(ex[s][:, 2, :, :], ex[s][:, 2, :, :], bc(gates[:, :, 2], 2, 64), ALU.mult).then_inc(pair_ready, 1)
                        v.wait_ge(pair_ready, 2 * n + 1)
                        nc.vector.tensor_tensor(hb[s][:, :, :], hb[s][:, :, :], ex[s][:, 2, :, :], ALU.add).then_inc(pair_ready, 1)
                        v.wait_ge(third_ready, n + 1)
                        v.wait_ge(pair_ready, 2 * n + 2)
                        nc.vector.tensor_tensor(hb[s][:, :, :], hb[s][:, :, :], ex[s][:, 3, :, :], ALU.add).then_inc(half_ready, 1)
            assert k_used == K, k_used


def tensors(nc, ctx):
    sb = lambda n, s, d=F32: ctx.enter_context(nc.sbuf_tensor(n, s, d))
    return dict(ident=sb("ident", [128, 128]), ones=sb("ones", [128, 128]), before=sb("before", [128, 128]),
                halves=sb("halves", [128, 128]), stat_w=sb("stat_w", [128, 4]), reset=sb("reset", [128, 8, 32]),
                rowbase=sb("rowbase", [128, 32]), bias_s=sb("bias_s", [128, 1]), bound=sb("bound", [128, 1]),
                w_cat=sb("w_cat", [64, ROW]), w12=sb("w12", [128, 64]), bias4=sb("bias4", [1, 256]),
                m0=sb("m0", [128, 1]), unit=sb("unit", [128, ROW]),
                first_edge=sb("first_edge", [128, NODE_TILES], I32), last_edge=sb("last_edge", [128, NODE_TILES], I32),
                busy=sb("busy", [1, NODE_TILES // SKIP_GROUP], I32))


def program(nc, dram):
    with ExitStack() as ctx:
        t = tensors(nc, ctx)
        make_constants(nc, t, dram)
        select_and_sort(nc, t, dram)
        attend(nc, t, dram)
        with nc.sbuf_tensor("edge_rows", [128, NODE_TILES * ROW], F32) as rows:
            t["edge_rows"] = rows
            pass_messages(nc, t, dram)
            combine(nc, t, dram)


SCRATCH = {"kept": ((M_NODES, 64), F32), "lag_rows": ((128, 64, LAG_W), F32), "h2": ((32, 128, 16, 64), F32),
           "node": ((M_NODES, ROW), F32), "node_own": ((32, 128, 16, ROW), F32), "x3t": ((64, M_NODES), F32),
           "sort_scratch": ((2, 128, COLS), U16), "sorted_dst": ((128, COLS), U16), "sorted_src": ((128, COLS), I32),
           "edge_ad": ((N_EDGES, 4), F32), "runs": ((N_EDGES, ROW), F32), "experts": ((32, 128, 4096), F32),
           "tails": ((128, ROW), F32), "carries": ((128, ROW), F32), "nothing": ((2, NODE_TILES // SKIP_GROUP, 1), I32)}
INPUTS = {"x": "x", "norm_w": "L0_tok_norm_w", "norm_b": "L0_tok_norm_b", "fc_w": "L0_tok_fc_w", "fc_b": "L0_tok_fc_b",
          "A_W1": "L0_attn_W1", "A_W2": "L0_attn_W2", "A_bias": "L0_attn_bias", "mem": "L0_attn_memory_weights",
          "W_gat": "L0_ffn_W_gat", "att_src": "L0_ffn_att_src", "att_dst": "L0_ffn_att_dst", "b_gat": "L0_ffn_b_gat",
          "ln_gamma": "L0_ffn_ln_gamma", "ln_beta": "L0_ffn_ln_beta", "F_W1": "L0_ffn_W1", "F_b1": "L0_ffn_b1",
          "F_W2": "L0_ffn_W2", "F_b2": "L0_ffn_b2", "edges": "L0_ffn_edge_index"}


def kernel(**inputs):
    import numpy as _np
    import concourse.bacc as _bacc
    from concourse import mybir as _mybir
    from concourse.bass_utils import run_bass_kernel_spmd as _run

    nc = _bacc.Bacc("TRN2", target_bir_lowering=False, num_devices=1)
    arrays, dram = {}, {}
    for name, given in INPUTS.items():
        a = _np.ascontiguousarray(inputs[given])
        arrays[f"in_{name}"] = a
        dram[name] = nc.dram_tensor(f"in_{name}", a.shape, _mybir.dt.from_np(a.dtype), kind="ExternalInput").ap()
    for name, (shape, dt) in SCRATCH.items():
        dram[name] = nc.dram_tensor(name, shape, dt, kind="Internal").ap()
    dram["out"] = nc.dram_tensor("out_0", (32, 2048, 64), F32, kind="ExternalOutput").ap()
    program(nc, dram)
    r = _run(nc, [arrays], core_ids=[0])
    return r.results[0]["out_0"]
```
